# Optimizing a Trainium2 kernel written in Bass

```python
import numpy as np
import jax
import jax.numpy as jnp

def _softmax(x, axis=-1):
    return jax.nn.softmax(x, axis=axis)

def _gelu(x):
    return jax.nn.gelu(x, approximate=True)

def _silu(x):
    return jax.nn.silu(x)

def _sigmoid(x):
    return jax.nn.sigmoid(x)

def _layernorm(x, axis=-1, eps=1e-05):
    m = jnp.mean(x, axis=axis, keepdims=True)
    v = jnp.var(x, axis=axis, keepdims=True)
    return (x - m) / jnp.sqrt(v + eps)

def _scatter_add(tgt, idx, src, axis=0):
    return tgt.at[idx].add(src)

def _segment_sum(src, seg, n):
    return jax.ops.segment_sum(src, seg, n)
kernel_name = 'mk_dlrm_tower_d1_rec_r8_af98e5'

def setup_inputs(seed: int=0):
    np.random.seed(seed)
    _w = jnp.asarray

    def _rec_inputs():
        import jax
        import jax.numpy as jnp
        _tk = jax.random.key(seed)
        dense_ctx = jax.random.normal(jax.random.fold_in(_tk, 190), (2048, 16), jnp.float32)
        ids = jnp.stack([jax.random.randint(jax.random.fold_in(_tk, 200 + f), (2048,), 0, v, jnp.int32) for f, v in enumerate([1250, 1000, 1250, 1250, 1250, 1250, 1250, 12500])], axis=1)
        tbl_0 = 0.05 * jax.random.normal(jax.random.fold_in(_tk, 500 + 0), (1250, 1024), jnp.float32)
        tbl_1 = 0.05 * jax.random.normal(jax.random.fold_in(_tk, 500 + 1), (1000, 1024), jnp.float32)
        tbl_2 = 0.05 * jax.random.normal(jax.random.fold_in(_tk, 500 + 2), (1250, 1024), jnp.float32)
        tbl_3 = 0.05 * jax.random.normal(jax.random.fold_in(_tk, 500 + 3), (1250, 1024), jnp.float32)
        tbl_4 = 0.05 * jax.random.normal(jax.random.fold_in(_tk, 500 + 4), (1250, 1024), jnp.float32)
        tbl_5 = 0.05 * jax.random.normal(jax.random.fold_in(_tk, 500 + 5), (1250, 1024), jnp.float32)
        tbl_6 = 0.05 * jax.random.normal(jax.random.fold_in(_tk, 500 + 6), (1250, 1024), jnp.float32)
        tbl_7 = 0.05 * jax.random.normal(jax.random.fold_in(_tk, 500 + 7), (12500, 1024), jnp.float32)
        _rk = jax.random.fold_in(_tk, 7)
        W_top1 = 0.0310087 * jax.random.normal(jax.random.fold_in(_tk, 801), (1040, 512), jnp.float32)
        W_top2 = 0.0441942 * jax.random.normal(jax.random.fold_in(_tk, 802), (512, 256), jnp.float32)
        W_top3 = 0.0625 * jax.random.normal(jax.random.fold_in(_tk, 803), (256, 1), jnp.float32)
        b_top1 = jnp.zeros((512,), jnp.float32)
        b_top2 = jnp.zeros((256,), jnp.float32)
        return (dense_ctx, ids, tbl_0, tbl_1, tbl_2, tbl_3, tbl_4, tbl_5, tbl_6, tbl_7, W_top1, b_top1, W_top2, b_top2, W_top3)
    dense_ctx, ids, tbl_0, tbl_1, tbl_2, tbl_3, tbl_4, tbl_5, tbl_6, tbl_7, W_top1, b_top1, W_top2, b_top2, W_top3 = _rec_inputs()

    def _L0_rec_setup():
        import jax, jax.numpy as jnp
        import numpy as np
        B, F, H = (1024, 8, 1024)

        def _linear_params(key, fan_in, fan_out):
            kw, kb = jax.random.split(key)
            w = jax.random.normal(kw, (fan_in, fan_out), dtype=jnp.float32) * 0.02
            b = jax.random.normal(kb, (fan_out,), dtype=jnp.float32) * 0.02
            return (w, b)
        key = jax.random.key(seed)
        ks = jax.random.split(key, 7)
        field_vectors = jax.random.normal(ks[0], (B, F, H), dtype=jnp.float32)
        Wn1, bn1 = _linear_params(ks[1], H, H)
        Wn2, bn2 = _linear_params(ks[2], H, H)
        Wa1, ba1 = _linear_params(ks[3], 2 * H, H)
        Wa2, ba2 = _linear_params(ks[4], H, H)
        Wo1, bo1 = _linear_params(ks[5], 2 * H, H)
        Wo2, bo2 = _linear_params(ks[6], H, H)
        not_idx = jnp.array([2, 3], dtype=jnp.int64)
        and_pairs = jnp.array([[0, 1], [2, 3]], dtype=jnp.int64)
        or_pairs = jnp.array([[4, 5]], dtype=jnp.int64)
        return {'field_vectors': field_vectors, 'Wn1': Wn1, 'bn1': bn1, 'Wn2': Wn2, 'bn2': bn2, 'Wa1': Wa1, 'ba1': ba1, 'Wa2': Wa2, 'ba2': ba2, 'Wo1': Wo1, 'bo1': bo1, 'Wo2': Wo2, 'bo2': bo2, 'not_idx': not_idx, 'and_pairs': and_pairs, 'or_pairs': or_pairs}
    _L0_rec_all = _L0_rec_setup()
    _L0_rec_in = {k: v for k, v in _L0_rec_all.items() if k in ('Wn1', 'bn1', 'Wn2', 'bn2', 'Wa1', 'ba1', 'Wa2', 'ba2', 'Wo1', 'bo1', 'Wo2', 'bo2', 'not_idx', 'and_pairs', 'or_pairs')}
    del _L0_rec_all
    return {'dense_ctx': dense_ctx, 'ids': ids, 'tbl_0': tbl_0, 'tbl_1': tbl_1, 'tbl_2': tbl_2, 'tbl_3': tbl_3, 'tbl_4': tbl_4, 'tbl_5': tbl_5, 'tbl_6': tbl_6, 'tbl_7': tbl_7, 'W_top1': W_top1, 'b_top1': b_top1, 'W_top2': W_top2, 'b_top2': b_top2, 'W_top3': W_top3, 'L0_rec_Wn1': _L0_rec_in['Wn1'], 'L0_rec_bn1': _L0_rec_in['bn1'], 'L0_rec_Wn2': _L0_rec_in['Wn2'], 'L0_rec_bn2': _L0_rec_in['bn2'], 'L0_rec_Wa1': _L0_rec_in['Wa1'], 'L0_rec_ba1': _L0_rec_in['ba1'], 'L0_rec_Wa2': _L0_rec_in['Wa2'], 'L0_rec_ba2': _L0_rec_in['ba2'], 'L0_rec_Wo1': _L0_rec_in['Wo1'], 'L0_rec_bo1': _L0_rec_in['bo1'], 'L0_rec_Wo2': _L0_rec_in['Wo2'], 'L0_rec_bo2': _L0_rec_in['bo2'], 'L0_rec_not_idx': _L0_rec_in['not_idx'], 'L0_rec_and_pairs': _L0_rec_in['and_pairs'], 'L0_rec_or_pairs': _L0_rec_in['or_pairs']}

def reference(dense_ctx, ids, tbl_0, tbl_1, tbl_2, tbl_3, tbl_4, tbl_5, tbl_6, tbl_7, W_top1, b_top1, W_top2, b_top2, W_top3, L0_rec_Wn1, L0_rec_bn1, L0_rec_Wn2, L0_rec_bn2, L0_rec_Wa1, L0_rec_ba1, L0_rec_Wa2, L0_rec_ba2, L0_rec_Wo1, L0_rec_bo1, L0_rec_Wo2, L0_rec_bo2, L0_rec_not_idx, L0_rec_and_pairs, L0_rec_or_pairs):
    import jax
    import jax.numpy as jnp

    def _L0_rec_ref(field_vectors, Wn1, bn1, Wn2, bn2, Wa1, ba1, Wa2, ba2, Wo1, bo1, Wo2, bo2, not_idx, and_pairs, or_pairs):
        import jax, jax.numpy as jnp
        import numpy as np
        B, F, H = (1024, 8, 1024)

        def _linear_params(key, fan_in, fan_out):
            kw, kb = jax.random.split(key)
            w = jax.random.normal(kw, (fan_in, fan_out), dtype=jnp.float32) * 0.02
            b = jax.random.normal(kb, (fan_out,), dtype=jnp.float32) * 0.02
            return (w, b)
        num_fields = field_vectors.shape[1]
        x_not = jnp.take(field_vectors, not_idx, axis=1)
        t = jnp.tanh(jax.nn.relu(x_not @ Wn1 + bn1) @ Wn2 + bn2)
        iv = field_vectors.at[:, not_idx, :].set(t)

        def pair_fuse(pairs, W1, b1, W2, b2):
            v = jnp.concatenate([jnp.take(iv, pairs[:, 0], axis=1), jnp.take(iv, pairs[:, 1], axis=1)], axis=-1)
            return jax.nn.relu(v @ W1 + b1) @ W2 + b2
        and_out = pair_fuse(and_pairs, Wa1, ba1, Wa2, ba2)
        or_out = pair_fuse(or_pairs, Wo1, bo1, Wo2, bo2)
        processed = jnp.zeros((num_fields,), dtype=field_vectors.dtype).at[and_pairs.reshape(-1)].set(1.0).at[or_pairs.reshape(-1)].set(1.0)
        remaining = 1.0 - processed
        sum_res = and_out.sum(axis=1) + or_out.sum(axis=1) + jnp.einsum('bfh,f->bh', iv, remaining)
        count = and_pairs.shape[0] + or_pairs.shape[0] + remaining.sum()
        return sum_res / count
    e = jnp.stack([tbl_0[ids[:, 0]], tbl_1[ids[:, 1]], tbl_2[ids[:, 2]], tbl_3[ids[:, 3]], tbl_4[ids[:, 4]], tbl_5[ids[:, 5]], tbl_6[ids[:, 6]], tbl_7[ids[:, 7]]], axis=1)
    z = _L0_rec_ref(e, L0_rec_Wn1, L0_rec_bn1, L0_rec_Wn2, L0_rec_bn2, L0_rec_Wa1, L0_rec_ba1, L0_rec_Wa2, L0_rec_ba2, L0_rec_Wo1, L0_rec_bo1, L0_rec_Wo2, L0_rec_bo2, L0_rec_not_idx, L0_rec_and_pairs, L0_rec_or_pairs)
    z = z.reshape(z.shape[0], -1)
    h = jnp.concatenate([z, dense_ctx], axis=1)
    h = jnp.maximum(h @ W_top1 + b_top1, 0.0)
    h = jnp.maximum(h @ W_top2 + b_top2, 0.0)
    y = h @ W_top3
    return y

_drawn_inputs = setup_inputs


def setup_inputs(seed=0):
    import zlib

    import numpy as np

    out = dict(_drawn_inputs(seed))
    spreads = {'b_top1': (0.0, 0.1), 'b_top2': (0.0, 0.1)}
    factors = {'tbl_0': 4.516,
     'tbl_1': 4.533,
     'tbl_2': 8.0,
     'tbl_3': 8.0,
     'tbl_4': 4.603,
     'tbl_5': 4.631,
     'L0_rec_Wn1': 8.0,
     'L0_rec_bn1': 8.0,
     'L0_rec_Wn2': 8.0,
     'L0_rec_bn2': 8.0,
     'L0_rec_Wa1': 2.999,
     'L0_rec_ba1': 4.072,
     'L0_rec_Wo1': 3.474,
     'L0_rec_bo1': 8.0,
     'L0_rec_Wo2': 2.755}
    for name, (base, spread) in spreads.items():
        noise = np.random.default_rng([zlib.crc32(name.encode()), seed]).standard_normal(out[name].shape)
        drawn = base * np.exp(spread * noise) if base else spread * noise
        out[name] = jnp.asarray(drawn.astype(out[name].dtype))
    for name, factor in factors.items():
        out[name] = (out[name] * factor).astype(out[name].dtype)
    return out
```

```python
from contextlib import ExitStack

import concourse.bass as bass
from concourse import mybir

F32 = mybir.dt.float32
F32R = mybir.dt.float32r
I32 = mybir.dt.int32
U32 = mybir.dt.uint32
ALU = mybir.AluOpType
ACT = mybir.ActivationFunctionType
AX = mybir.AxisListType

P = 128
H = 1024
KB = H // P
N1, N2 = 512, 256
M1, M2 = N1 // P, N2 // P
BATCH = 2048
FIELDS = 8
DENSE = 16
VOCAB = [1250, 1000, 1250, 1250, 1250, 1250, 1250, 12500]
NOTS, ANDS, ORS = [2, 3], [0, 1, 2, 3], [4, 5]
STRUCTURE = NOTS + ANDS + ORS
PAIRS = (len(ANDS) + len(ORS)) // 2

COLS = 256
WIDE = 512
FIELD_ORDER = [4, 5, 2, 3, 0, 1]
PIECES = {f: -(-VOCAB[f] // COLS) for f in FIELD_ORDER}
FIRST_PIECE, _at = {}, 0
for _f in FIELD_ORDER:
    FIRST_PIECE[_f] = _at
    _at += PIECES[_f]
FIRST_PIECE["Wa2"] = _at
FIRST_PIECE["Wo2"] = _at + H // COLS
TOTAL_PIECES = _at + 2 * (H // COLS)

CHUNK = 512
CHUNKS = BATCH // CHUNK
TILES = CHUNK // P
SOURCES = 3

COL_BN1, COL_BN2, COL_BA2, COL_BO2 = 0, KB, 2 * KB, 3 * KB
COL_BT1 = 4 * KB
COL_BT2 = COL_BT1 + M1
COL_WT3 = COL_BT2 + M2
NCOLS = COL_WT3 + M2


def repeat(engine, first, count, body, period=2):
    rounds = count // period
    done = 0
    if rounds >= 2:
        with engine.Fori(0, rounds) as r:
            for s in range(period):
                body(r, first + s)
        done = rounds * period
    for i in range(first + done, first + count):
        body(0, i)


class Segment:

    def __init__(self, kind, weights, source, piece, units, target, bias=None, func=None):
        self.kind = kind
        self.weights = weights
        self.source, self.piece = source, piece
        self.units, self.target, self.bias, self.func = units, target, bias, func
        self.pieces_per_unit = 2 if kind == "columns" else 1
        self.groups_per_unit = {"rows": 4, "columns": 8, "fold": 2}[kind]

    def place(self, unit, group, piece):
        self.unit0, self.group0, self.piece0 = unit, group, piece
        self.unit_end = unit + self.units
        self.group_end = group + self.units * self.groups_per_unit
        self.pieces = self.units * self.pieces_per_unit
        self.piece_end = piece + self.pieces
        return self.unit_end, self.group_end, self.piece_end


def read_structure(nc, ctx, not_idx, and_pairs, or_pairs):
    keep = lambda name, shape, dt: ctx.enter_context(nc.sbuf_tensor(name, shape, dt))
    flag = keep("flag", [P, 1], I32)
    picks_i = keep("picks_i", [P, len(STRUCTURE)], I32)
    remaining = keep("remaining", [P, FIELDS], F32)
    inv_count = keep("inv_count", [P, 1], F32)
    with ExitStack() as inner:
        _read_structure(nc, inner, not_idx, and_pairs, or_pairs, picks_i, flag, remaining, inv_count)
    return picks_i, flag, remaining, inv_count


def _read_structure(nc, ctx, not_idx, and_pairs, or_pairs, picks_i, flag, remaining, inv_count):
    sb = lambda name, shape, dt: ctx.enter_context(nc.sbuf_tensor(name, shape, dt))
    n, npair = len(STRUCTURE), len(ANDS) + len(ORS)
    picks = sb("picks", [P, n], F32)
    expected = sb("expected", [P, n], F32)
    field_no = sb("field_no", [P, FIELDS], F32)
    differ = sb("differ", [P, n], F32)
    differ_any = sb("differ_any", [P, 1], F32)
    hits = sb("hits", [P, npair, FIELDS], F32)
    processed = sb("processed", [P, FIELDS], F32)
    count = sb("count", [P, 1], F32)
    count_all = sb("count_all", [P, 1], F32)
    picks_landed = ctx.enter_context(nc.semaphore("picks_landed"))
    step = ctx.enter_context(nc.semaphore("structure_step"))

    with nc.Block() as block:

        @block.sync
        def _(sp):
            sp.dma_start(picks_i[:, 0:2], not_idx.partition_broadcast(P)).then_inc(picks_landed, 16)
            sp.dma_start(picks_i[:, 2:6], and_pairs.rearrange("a b -> (a b)").partition_broadcast(P)).then_inc(picks_landed, 16)
            sp.dma_start(picks_i[:, 6:8], or_pairs.rearrange("a b -> (a b)").partition_broadcast(P)).then_inc(picks_landed, 16)

        @block.vector
        def _(dve):
            for i, v in enumerate(STRUCTURE):
                dve.memset(expected[:, i:i + 1], float(v)).then_inc(step, 1)
            for f in range(FIELDS):
                dve.memset(field_no[:, f:f + 1], float(f)).then_inc(step, 1)
            at = n + FIELDS
            dve.wait_ge(picks_landed, 48)
            dve.tensor_copy(picks[:], picks_i[:]).then_inc(step, 1)
            dve.wait_ge(step, at + 1)
            dve.tensor_tensor(differ[:], picks[:], expected[:], ALU.not_equal).then_inc(step, 1)
            for e in range(npair):
                dve.tensor_scalar(hits[:, e, :], field_no[:], picks[:, 2 + e:3 + e], None,
                                  ALU.is_equal).then_inc(step, 1)
            dve.wait_ge(step, at + 2 + npair)
            dve.tensor_reduce(differ_any[:], differ[:], AX.X, ALU.max).then_inc(step, 1)
            dve.tensor_reduce(processed[:], hits[:].rearrange("p e f -> p f e"), AX.X,
                              ALU.max).then_inc(step, 1)
            dve.wait_ge(step, at + 4 + npair)
            dve.tensor_copy(flag[:], differ_any[:]).then_inc(step, 1)
            dve.tensor_scalar(remaining[:], processed[:], -1.0, 1.0, ALU.mult, ALU.add).then_inc(step, 1)
            dve.wait_ge(step, at + 6 + npair)
            dve.tensor_reduce(count[:], remaining[:], AX.X, ALU.add).then_inc(step, 1)
            dve.wait_ge(step, at + 7 + npair)
            dve.tensor_scalar(count_all[:], count[:], float(PAIRS), None, ALU.add).then_inc(step, 1)
            dve.wait_ge(step, at + 8 + npair)
            dve.reciprocal(inv_count[:], count_all[:]).then_inc(step, 1)
            dve.wait_ge(step, at + 9 + npair)


def table_path(nc, inv_count, t):
    with ExitStack() as ctx:
        sb = lambda name, shape, dt=F32: ctx.enter_context(nc.sbuf_tensor(name, shape, dt))
        sem = lambda name: ctx.enter_context(nc.semaphore(name))
        dram = lambda name, shape: nc.dram_tensor(name, shape, F32, kind="Internal").ap()

        hidden_t = dram("hidden_t", [2 * PIECES[2], P, KB, COLS])
        tanh_t = dram("tanh_t", [2 * PIECES[2], P, KB, COLS])
        half = {f: dram(f"half_{f}", [PIECES[f] * COLS, H]) for f in FIELD_ORDER}

        w_hi, w_lo = sb("w_hi", [P, KB, H], F32R), sb("w_lo", [P, KB, H], F32R)
        z_hi, z_lo = sb("z_hi", [P, KB, N1], F32R), sb("z_lo", [P, KB, N1], F32R)
        x_hi = sb("x_hi", [P, 2, KB, WIDE], F32R)
        x_lo = sb("x_lo", [P, 2, KB, WIDE], F32R)
        b2_parts = sb("b2_parts", [P, KB, 2], F32R)
        stage = sb("stage", [P, 4 * 2 * H])
        x_raw = stage[:, 0:2 * KB * COLS].rearrange("p (s k c) -> p s k c", s=2, k=KB)
        w_raw = stage[:, 2 * KB * COLS:2 * KB * COLS + 3 * H].rearrange("p (s k c) -> p s k c", s=3, k=KB)
        bias_row = stage[:, 7 * H:8 * H]
        looked = stage[:, :].rearrange("p (s two n) -> p s two n", s=4, two=2)
        small = sb("small", [P, 7, WIDE])
        out_ring = small[:, 0:4, :]
        top_ring = small[:, 0:3, :]
        wt2 = small[:, 3:5, :].rearrange("p a b -> p (a b)").rearrange("p (k n) -> p k n", k=M1)
        wt1_dense = small[:, 5, :]
        dense_t = small[:, 6, :]
        identity = sb("identity", [P, P])
        columns = sb("columns", [P, NCOLS])
        b2 = sb("b2", [P, KB])
        bias1 = sb("bias1", [P, M1])
        ids = sb("ids", [P, CHUNKS, TILES * FIELDS], I32)
        ids_now = sb("ids_now", [P, 2, TILES * FIELDS], I32)

        bank = [ctx.enter_context(nc.psum_tensor(f"bank{i}", [P, WIDE], F32)) for i in range(8)]

        x_src = t["x_pieces"]
        segments = [
            Segment("rows", 0, x_src, FIRST_PIECE[4], PIECES[4], half[4], bias="bo1"),
            Segment("rows", 1, x_src, FIRST_PIECE[5], PIECES[5], half[5]),
            Segment("columns", 2, x_src, FIRST_PIECE[2], PIECES[2], hidden_t, func=(ACT.Relu, COL_BN1)),
            Segment("columns", 3, hidden_t, 0, PIECES[2], tanh_t, func=(ACT.Tanh, COL_BN2)),
            Segment("rows", 4, x_src, FIRST_PIECE[0], PIECES[0], half[0], bias="ba1"),
            Segment("rows", 4, tanh_t, 0, PIECES[2], half[2], bias="ba1"),
            Segment("rows", 5, tanh_t, PIECES[2], PIECES[3], half[3]),
            Segment("rows", 5, x_src, FIRST_PIECE[1], PIECES[1], half[1]),
            Segment("fold", 6, x_src, FIRST_PIECE["Wa2"], H // COLS, 0),
            Segment("fold", 6, x_src, FIRST_PIECE["Wo2"], H // COLS, 1),
        ]
        u = g = q = 0
        for s in segments:
            u, g, q = s.place(u, g, q)
        UNITS, GROUPS, ALL_PIECES = u, g, q
        STORED_GROUPS = segments[7].group_end
        made_by = {id(hidden_t): segments[2], id(tanh_t): segments[3]}
        last_of = {s.weights: s for s in segments}
        first_of = {s.weights: s for s in reversed(segments)}
        BLOCKS = [KB] * 6 + [M1]
        block0 = [sum(BLOCKS[:i]) for i in range(len(BLOCKS) + 1)]
        BIASED = {}
        n = 0
        for i, s in enumerate(segments):
            BIASED[i] = n
            if s.bias:
                n += s.units * s.groups_per_unit
        BIASED_ALL = n
        first_and = [s.bias for s in segments].index("ba1")

        x_landed = [sem(f"x_landed{i}") for i in range(2)]
        x_rounded = sem("x_rounded")
        x_split = sem("x_split")
        w_landed = [sem(f"w_landed{i}") for i in range(3)]
        w_scaled = sem("w_scaled")
        w_rounded = sem("w_rounded")
        w_split = sem("w_split")
        products = sem("products")
        bank_free = sem("bank_free")
        fold_rounded = sem("fold_rounded")
        fold_split = sem("fold_split")
        bias_landed = sem("bias_landed")
        biased = sem("biased")
        stored = [sem(f"stored{i}") for i in range(4)]
        consts_landed = sem("consts_landed")
        identity_ready = sem("identity_ready")
        b2_step = sem("b2_step")
        b2_product = sem("b2_product")
        top_landed = sem("top_landed")
        dense_landed = sem("dense_landed")
        dense_used = sem("dense_used")
        ids_ready = sem("ids_ready")
        looked_up = [sem(f"looked_up{i}") for i in range(4)]
        slot_taken = sem("slot_taken")
        added = sem("added")
        first_added = sem("first_added")
        relued = sem("relued")
        summed = sem("summed")
        and_summed = sem("and_summed")
        turned = sem("turned")
        turned_hi = sem("turned_hi")
        turned_lo = sem("turned_lo")
        h1_done, h1_out = sem("h1_done"), sem("h1_out")
        h1_used = sem("h1_used")
        h2_done, h2_out = sem("h2_done"), sem("h2_out")
        y_done, y_out = sem("y_done"), sem("y_out")
        y_stored = sem("y_stored")
        y_free = sem("y_free")

        C_UNIT = UNITS % 2
        PER_CHUNK = SOURCES * TILES * 2
        REMAINING, OR, AND = range(SOURCES)

        def rows_of(dst):
            return dst.rearrange("(n p) c -> n p c", p=P)

        with nc.Block() as block:

            @block.sync
            def _(sp):
                def load_weights(w, blocks):
                    for b in blocks:
                        n = block0[w] + b
                        if n >= 3:
                            sp.wait_ge(w_split, n - 2)
                        sp.dma_start(w_raw[:, n % 3], t["w_blocks"][n]).then_inc(w_landed[n % 3], 16)

                def load_piece(s, r, k):
                    q = s.piece0 + k
                    if not (isinstance(r, int) and q < 2):
                        sp.wait_ge(x_split, r * 2 + (q - 1))
                    made = made_by.get(id(s.source))
                    if made is not None:
                        unit = (s.piece + k) // 2
                        for ring in range(4):
                            sp.wait_ge(stored[ring], r * (16 * 2) + 16 * (made.group0 + 8 * (unit + 1)) // 4)
                    sp.dma_start(x_raw[:, q % 2], s.source[r * 2 + (s.piece + k)]).then_inc(x_landed[q % 2], 16)

                sp.sem_inc(y_free, 1)
                load_weights(0, range(0, 3))
                for k in range(2):
                    load_piece(segments[0], 0, k)
                load_weights(0, range(3, BLOCKS[0]))
                for i, s in enumerate(segments):
                    w = s.weights
                    if first_of[w] is s and w + 1 < len(BLOCKS):
                        load_weights(w + 1, range(0, 3))
                    repeat(sp, 2, s.pieces - 2, lambda r, k: load_piece(s, r, k))
                    if i + 1 < len(segments):
                        for k in range(2):
                            load_piece(segments[i + 1], 0, k)
                    if last_of[w] is s and w + 1 < len(BLOCKS):
                        load_weights(w + 1, range(3, BLOCKS[w + 1]))
                sp.wait_ge(stored[3], 16 * STORED_GROUPS // 4)
                sp.dma_start(wt2, t["wt2"]).then_inc(top_landed, 16)
                sp.dma_start(wt1_dense[0:DENSE, :], t["W_top1"][H:H + DENSE, :]).then_inc(top_landed, 16)

                def chunk(r, c):
                    sp.wait_ge(dense_used, r * 2 + (c + 1))
                    sp.dma_start(dense_t[0:DENSE, :], t["dense_t"][r * 2 + c]).then_inc(dense_landed, 16)
                    sp.wait_ge(y_out, r * 2 + (c + 1))
                    sp.dma_start(t["y"][r * 2 + c], top_ring[0:1, 0, :]).then_inc(y_stored, 16)
                    sp.wait_ge(y_stored, r * 32 + 16 * (c + 1))
                    sp.sem_inc(y_free, 1)
                repeat(sp, 0, CHUNKS, chunk)
                sp.wait_ge(y_stored, 16 * CHUNKS)

            @block.gpsimd
            def _(pool):
                pool.memset(identity[:], 0.0).then_inc(identity_ready, 1)
                pool.wait_ge(identity_ready, 1)
                pool.affine_select(out=identity[:], in_=identity[:], compare_op=ALU.not_equal, fill=1.0,
                                   base=0, pattern=[[-1, P]], channel_multiplier=1).then_inc(identity_ready, 1)
                for w, blocks in enumerate(BLOCKS):
                    top = w == len(BLOCKS) - 1
                    hi, lo = (z_hi, z_lo) if top else (w_hi, w_lo)
                    for b in range(blocks):
                        n = block0[w] + b
                        raw = w_raw[:, n % 3]
                        cols = slice(b * P, (b + 1) * P)
                        pool.wait_ge(w_landed[n % 3], 16 * (n // 3 + 1))
                        if top:
                            pool.tensor_scalar(raw, raw, inv_count[:, 0:1], None, ALU.mult).then_inc(w_scaled, 1)
                            pool.wait_ge(w_scaled, b + 1)
                        elif w:
                            before = last_of[w - 1]
                            if before.kind == "columns":
                                pool.wait_ge(products, before.group_end - KB + b + 1)
                            else:
                                pool.wait_ge(products, before.group_end - (2 if b < KB // 2 else 0))
                        pool.tensor_copy(hi[:, :, cols], raw).then_inc(w_rounded, 1)
                        pool.wait_ge(w_rounded, n + 1)
                        pool.tensor_tensor(lo[:, :, cols], raw, hi[:, :, cols], ALU.subtract).then_inc(w_split, 1)

                pool.wait_ge(w_split, block0[-1])
                pool.wait_ge(x_split, ALL_PIECES)
                pool.wait_ge(biased, BIASED_ALL)
                pool.wait_ge(consts_landed, 16 * 2)
                for ring in range(4):
                    pool.wait_ge(stored[ring], 16 * STORED_GROUPS // 4)

                def lookup(slot, c, tile, fields):
                    pool.sem_inc(slot_taken, 1)
                    for j, f in enumerate(fields):
                        index = ids_now[:, c % 2, tile * FIELDS + f:tile * FIELDS + f + 1]
                        src = t["tables"][f] if f >= 6 else half[f]
                        pool.indirect_dma_start(
                            out=looked[:, slot, j, :], out_offset=None, in_=src,
                            in_offset=bass.IndirectOffsetOnAxis(ap=index.bitcast(U32), axis=0),
                            bounds_check=src.shape[0] - 1, oob_is_err=False,
                        ).then_inc(looked_up[slot], 16)

                def chunk(r, c):
                    pool.tensor_copy(ids_now[:, c % 2, :], ids[:, r * 2 + c, :]).then_inc(ids_ready, 1)
                    pool.wait_ge(ids_ready, r * 2 + (c + 1))
                    base = PER_CHUNK * (c + 1)
                    turned_at = lambda source, tile: r * (2 * PER_CHUNK) + (base + source * TILES * 2 + 2 * (tile + 1))
                    for tile in range(TILES):
                        if tile % 2 == 0:
                            pool.wait_ge(turned, r * (2 * PER_CHUNK) + (base - PER_CHUNK + AND * TILES * 2 + 2 * (2 + tile // 2 + 1)))
                        else:
                            pool.wait_ge(and_summed, r * 8 + 4 * c + (2 + tile // 2 + 1))
                        lookup(tile, c, tile, (6, 7))
                    for tile in range(TILES):
                        pool.wait_ge(turned, turned_at(REMAINING, tile))
                        lookup(tile, c, tile, (4, 5))
                    for tile in range(TILES):
                        for second, fields in enumerate(((0, 1), (2, 3))):
                            slot = (2 * tile + second) % 4
                            if tile < 2:
                                pool.wait_ge(turned, turned_at(OR, slot))
                            elif second:
                                pool.wait_ge(and_summed, r * 8 + 4 * (c + 1) + (tile - 2 + 1))
                            else:
                                pool.wait_ge(turned, turned_at(AND, tile - 2))
                            lookup(slot, c, tile, fields)
                repeat(pool, 0, CHUNKS, chunk)

            @block.scalar
            def _(act):
                act.dma_start(columns[:], t["columns"]).then_inc(consts_landed, 16)
                act.dma_start(ids[:], t["ids"]).then_inc(consts_landed, 16)
                act.dma_start(bias_row, t["bo1"].partition_broadcast(P)).then_inc(bias_landed, 16)
                act.sem_inc(bank_free, 4)
                act.sem_inc(h1_out, 4)
                act.wait_ge(consts_landed, 32)

                def evacuate(s, i, r, k, j):
                    per = s.groups_per_unit
                    g = s.group0 + k * per + j
                    ring = g % 4
                    act.wait_ge(products, r * (2 * per) + (g + 1))
                    if not (isinstance(r, int) and g < 4):
                        act.wait_ge(stored[ring], r * (16 * 2 * per // 4) + 16 * (g // 4))
                    if s.kind == "columns":
                        func, col = s.func
                        act.activation(out_ring[:, ring, :], bank[ring][:], func,
                                       bias=columns[:, col + j:col + j + 1]).then_inc(bank_free, 1)
                        dst = s.target.rearrange("(u a) p m c -> u m p a c", a=2)[r * 2 + k, j]
                        src = out_ring[:, ring, :].rearrange("p (a c) -> p a c", a=2)
                    else:
                        act.activation(out_ring[:, ring, :], bank[ring][:], ACT.Copy).then_inc(bank_free, 1)
                        side, tile = j // 2, j % 2
                        dst = rows_of(s.target)[r * 4 + (2 * k + tile), :, side * WIDE:(side + 1) * WIDE]
                        src = out_ring[:, ring, :]
                    if s.bias:
                        act.wait_ge(biased, r * (2 * per) + (BIASED[i] + k * per + j + 1))
                    else:
                        act.wait_ge(bank_free, r * (2 * per) + (4 + g + 1))
                    act.dma_start(dst, src).then_inc(stored[ring], 16)

                def fold(s, r, k, j):
                    g = s.group0 + k * 2 + j
                    act.wait_ge(products, r * 4 + (g + 1))
                    act.activation(w_hi[:, 2 * k + j, s.target * N1:(s.target + 1) * N1], bank[g % 4][:],
                                   ACT.Copy).then_inc(fold_rounded, 1)
                    act.wait_ge(fold_split, g - segments[8].group0 + 1)
                    act.sem_inc(bank_free, 1)

                for i, s in enumerate(segments):
                    if s.kind == "fold":
                        for k in range(s.units):
                            for j in range(2):
                                fold(s, 0, k, j)
                        continue
                    if i == first_and:
                        act.wait_ge(biased, BIASED[i])
                        act.dma_start(bias_row, t["ba1"].partition_broadcast(P)).then_inc(bias_landed, 16)
                    per = s.groups_per_unit
                    unit = lambda r, k: [evacuate(s, i, r, k, j) for j in range(per)]
                    if i == 0:
                        unit(0, 0)
                        repeat(act, 1, s.units - 1, unit)
                    else:
                        repeat(act, 0, s.units, unit)

                for ring in range(4):
                    act.wait_ge(stored[ring], 16 * STORED_GROUPS // 4)

                def turn_hi(r, c, source, tile):
                    func = ACT.Relu if source == OR else ACT.Copy
                    cb = (C_UNIT + SOURCES * c + source) % 2
                    for h in range(2):
                        n = PER_CHUNK * c + (source * TILES + tile) * 2 + h
                        act.wait_ge(turned, r * (2 * PER_CHUNK) + (PER_CHUNK + n + 1))
                        act.activation(x_hi[:, cb, 4 * h:4 * h + 4, tile * P:(tile + 1) * P],
                                       bank[4 + h][:].rearrange("p (b c) -> p b c", b=4), func).then_inc(turned_hi, 1)

                def relu_second(r, c, tile):
                    slot = (2 * tile + 1) % 4
                    act.wait_ge(added, r * 8 + 4 * c + (tile + 1))
                    act.activation(looked[:, slot, 0, :], looked[:, slot, 0, :], ACT.Relu).then_inc(relued, 1)

                def chunk(r, c):
                    order = [(source, tile) for source in range(SOURCES) for tile in range(TILES)]
                    for n, (source, tile) in enumerate(order):
                        if n + 1 < len(order) and order[n + 1][0] == AND:
                            relu_second(r, c, order[n + 1][1])
                        turn_hi(r, c, source, tile)
                    for m in range(M1):
                        act.wait_ge(h1_done, r * (2 * M1) + (M1 * c + m + 1))
                        if m == 0:
                            act.wait_ge(y_free, r * 2 + (c + 1))
                            act.wait_ge(b2_step, 4)
                        if m == 3:
                            act.wait_ge(h1_used, r * 2 + (c + 1))
                        act.activation(top_ring[:, m % 3, :], bank[m][:], ACT.Relu,
                                       bias=bias1[:, m:m + 1]).then_inc(h1_out, 1)
                    for m in range(M2):
                        act.wait_ge(h2_done, r * (2 * M2) + (M2 * c + m + 1))
                        act.activation(top_ring[:, 1 + m, :], bank[6 + m][:], ACT.Relu,
                                       bias=columns[:, COL_BT2 + m:COL_BT2 + m + 1]).then_inc(h2_out, 1)
                    act.wait_ge(y_done, r * 2 + (c + 1))
                    act.activation(top_ring[0:1, 0, :], bank[6][0:1, :], ACT.Copy).then_inc(y_out, 1)
                repeat(act, 0, CHUNKS, chunk)

            @block.vector
            def _(dve):
                dve.sem_inc(and_summed, 4)
                dve.sem_inc(turned_lo, 2)

                def split(s, r, k):
                    u = s.unit0 + k
                    buffer = u % 2
                    if not (isinstance(r, int) and u < 2):
                        per = s.groups_per_unit
                        if k >= 2:
                            dve.wait_ge(products, r * (2 * per) + (s.group0 + (k - 1) * per))
                        else:
                            before = segments[segments.index(s) - 1]
                            dve.wait_ge(products, before.group_end - (1 - k) * before.groups_per_unit)
                    for a in range(s.pieces_per_unit):
                        q = s.piece0 + k * s.pieces_per_unit + a
                        step = 2 * s.pieces_per_unit
                        cols = slice(a * COLS, (a + 1) * COLS)
                        dve.wait_ge(x_landed[q % 2], r * (16 * step // 2) + 16 * (q // 2 + 1))
                        dve.tensor_copy(x_hi[:, buffer, :, cols], x_raw[:, q % 2]).then_inc(x_rounded, 1)
                        dve.wait_ge(x_rounded, r * step + (q + 1))
                        dve.tensor_tensor(x_lo[:, buffer, :, cols], x_raw[:, q % 2], x_hi[:, buffer, :, cols],
                                          ALU.subtract).then_inc(x_split, 1)

                def add_bias(s, i, r, k):
                    for j in range(4):
                        g = s.group0 + k * 4 + j
                        side = j // 2
                        dve.wait_ge(bank_free, r * 8 + (4 + g + 1))
                        tile = out_ring[:, g % 4, :]
                        dve.tensor_tensor(tile, tile, bias_row[:, side * WIDE:(side + 1) * WIDE],
                                          ALU.add).then_inc(biased, 1)

                def fold_lo(s, k):
                    for j in range(2):
                        g = s.group0 + k * 2 + j
                        cols = slice(s.target * N1, (s.target + 1) * N1)
                        dve.wait_ge(fold_rounded, g - segments[8].group0 + 1)
                        dve.tensor_tensor(w_lo[:, 2 * k + j, cols], bank[g % 4][:], w_hi[:, 2 * k + j, cols],
                                          ALU.subtract).then_inc(fold_split, 1)

                for k in range(2):
                    split(segments[0], 0, k)
                for i, s in enumerate(segments):
                    if s.bias:
                        dve.wait_ge(bias_landed, 16 if s.bias == "bo1" else 32)

                    def own(r, k):
                        if s.bias:
                            add_bias(s, i, r, k)
                        elif s.kind == "fold":
                            fold_lo(s, k)

                    def step(r, k):
                        own(r, k)
                        split(s, r, k + 2)
                    if s.kind == "fold":
                        for k in range(s.units - 2):
                            step(0, k)
                    else:
                        repeat(dve, 0, s.units - 2, step)
                    for k in range(2):
                        own(0, s.units - 2 + k)
                        if i + 1 < len(segments):
                            split(segments[i + 1], 0, k)

                dve.scalar_tensor_tensor(out=b2[:], in0=columns[:, COL_BA2:COL_BA2 + KB], scalar=float(len(ANDS) // 2),
                                         in1=columns[:, COL_BO2:COL_BO2 + KB], op0=ALU.mult, op1=ALU.add).then_inc(b2_step, 1)
                dve.wait_ge(b2_step, 1)
                dve.tensor_copy(b2_parts[:, :, 0], b2[:]).then_inc(b2_step, 1)
                dve.wait_ge(b2_step, 2)
                dve.tensor_tensor(b2_parts[:, :, 1], b2[:], b2_parts[:, :, 0], ALU.subtract).then_inc(b2_step, 1)
                dve.wait_ge(b2_product, 1)
                dve.tensor_reduce(bias1[:], bank[7][:, 0:2 * M1].rearrange("p (m two) -> p m two", two=2),
                                  AX.X, ALU.add).then_inc(b2_step, 1)
                dve.wait_ge(b2_step, 4)
                dve.tensor_tensor(bias1[:], bias1[:], columns[:, COL_BT1:COL_BT1 + M1], ALU.add).then_inc(b2_step, 1)

                def add_rows(r, c, source, tile):
                    if source != AND:
                        slots = [tile]
                        uses = [c * 4 + source]
                    else:
                        slots = [(2 * tile + 1) % 4, (2 * tile) % 4]
                        uses = [c * 4 + 2 + tile // 2] * 2
                    for n, slot in enumerate(slots):
                        dve.wait_ge(looked_up[slot], r * (32 * 8) + 32 * (uses[n] + 1))
                        a, b = looked[:, slot, 0, :], looked[:, slot, 1, :]
                        op = dve.tensor_tensor(a, a, b, ALU.add)
                        if source != AND:
                            op.then_inc(summed, 1)
                        elif n == 0:
                            op.then_inc(added, 1)
                        else:
                            op.then_inc(first_added, 1)
                            dve.wait_ge(first_added, r * 8 + 4 * c + (tile + 1))
                            dve.wait_ge(relued, r * 8 + 4 * c + (tile + 1))
                            dve.scalar_tensor_tensor(out=a, in0=a, scalar=0.0, in1=looked[:, slots[0], 0, :],
                                                     op0=ALU.max, op1=ALU.add).then_inc(and_summed, 1)

                def turn_lo(r, c, source, tile):
                    cb = (C_UNIT + SOURCES * c + source) % 2
                    for h in range(2):
                        n = PER_CHUNK * c + (source * TILES + tile) * 2 + h
                        where = (slice(None), cb, slice(4 * h, 4 * h + 4), slice(tile * P, (tile + 1) * P))
                        turned_bank = bank[4 + h][:].rearrange("p (b c) -> p b c", b=4)
                        dve.wait_ge(turned_hi, r * (2 * PER_CHUNK) + (n + 1))
                        if source == OR:
                            dve.scalar_tensor_tensor(out=x_lo[where], in0=turned_bank, scalar=0.0, in1=x_hi[where],
                                                     op0=ALU.max, op1=ALU.subtract).then_inc(turned_lo, 1)
                        else:
                            dve.tensor_tensor(x_lo[where], turned_bank, x_hi[where], ALU.subtract).then_inc(turned_lo, 1)

                def chunk(r, c):
                    order = [(source, tile) for source in range(SOURCES) for tile in range(TILES)]
                    add_rows(r, c, *order[0])
                    for n, at in enumerate(order):
                        if n + 1 < len(order):
                            add_rows(r, c, *order[n + 1])
                        turn_lo(r, c, *at)
                repeat(dve, 0, CHUNKS, chunk)

            @block.tensor
            def _(pe):
                pe.sem_inc(turned, PER_CHUNK)
                pe.sem_inc(dense_used, 1)

                def three_passes(out, stationary, moving, start, stop):
                    (s_hi, s_lo), (m_hi, m_lo) = stationary, moving
                    pe.matmul(out, s_hi, m_hi, start=start, stop=False)
                    pe.matmul(out, s_hi, m_lo, start=False, stop=False)
                    return pe.matmul(out, s_lo, m_hi, start=False, stop=stop)

                def unit(s, r, k):
                    per = s.groups_per_unit
                    buffer = (s.unit0 + k) % 2
                    pe.wait_ge(x_split, r * (2 * s.pieces_per_unit) + (s.piece0 + (k + 1) * s.pieces_per_unit))
                    for j in range(per):
                        g = s.group0 + k * per + j
                        pe.wait_ge(bank_free, r * (2 * per) + (g + 1))
                        if s.kind == "columns":
                            pe.wait_ge(w_split, block0[s.weights] + j + 1)
                        elif j == 0:
                            pe.wait_ge(w_split, block0[s.weights] + (KB // 2 if s.kind == "rows" else M1))
                        elif j == 2:
                            pe.wait_ge(w_split, block0[s.weights] + KB)
                        for kb in range(KB):
                            if s.kind == "columns":
                                cols = slice(j * P, (j + 1) * P)
                                stationary = w_hi[:, kb, cols], w_lo[:, kb, cols]
                                moving = x_hi[:, buffer, kb, :], x_lo[:, buffer, kb, :]
                            else:
                                side, tile = (j // 2, j % 2) if s.kind == "rows" else (0, j)
                                rows = slice(tile * P, (tile + 1) * P)
                                cols = slice(side * WIDE, (side + 1) * WIDE)
                                stationary = x_hi[:, buffer, kb, rows], x_lo[:, buffer, kb, rows]
                                moving = (w_hi[:, kb, cols], w_lo[:, kb, cols]) if s.kind == "rows" else (z_hi[:, kb, :], z_lo[:, kb, :])
                            last = three_passes(bank[g % 4][:], stationary, moving, kb == 0, kb == KB - 1)
                        last.then_inc(products, 1)

                for s in segments:
                    repeat(pe, 0, s.units, lambda r, k: unit(s, r, k))

                pe.wait_ge(b2_step, 3)
                for m in range(M1):
                    for kb in range(KB):
                        for part, z in enumerate((z_hi, z_lo)):
                            last = pe.matmul(bank[7][:, 2 * m:2 * m + 2], z[:, kb, m * P:(m + 1) * P], b2_parts[:, kb, :],
                                             start=(kb == 0 and part == 0), stop=(kb == KB - 1 and part == 1))
                last.then_inc(b2_product, 1)
                pe.wait_ge(bank_free, 4 + GROUPS)
                pe.wait_ge(identity_ready, 2)
                pe.wait_ge(top_landed, 32)
                pe.wait_ge(b2_step, 4)

                def turn(r, c, source, tile):
                    if source == AND:
                        pe.wait_ge(and_summed, r * 8 + 4 * c + (4 + tile + 1))
                        slot = (2 * tile) % 4
                    else:
                        pe.wait_ge(summed, r * (2 * 2 * TILES) + (c * 2 * TILES + source * TILES + tile + 1))
                        slot = tile
                    for h in range(2):
                        n = PER_CHUNK * c + (source * TILES + tile) * 2 + h
                        pe.wait_ge(turned_lo, r * (2 * PER_CHUNK) + (n + 1))
                        for b in range(4):
                            kb = 4 * h + b
                            last = pe.transpose(bank[4 + h][:, b * P:(b + 1) * P],
                                                looked[:, slot, 0, kb * P:(kb + 1) * P], identity[:])
                        last.then_inc(turned, 1)

                def multiply(r, c, source, m):
                    cb = (C_UNIT + SOURCES * c + source) % 2
                    hi, lo, at = [(z_hi, z_lo, 0), (w_hi, w_lo, N1), (w_hi, w_lo, 0)][source]
                    cols = slice(at + m * P, at + (m + 1) * P)
                    if m == 0:
                        pe.wait_ge(turned_lo, r * (2 * PER_CHUNK) + (2 + PER_CHUNK * c + (source + 1) * TILES * 2))
                    if source == REMAINING:
                        pe.wait_ge(h1_out, r * (2 * M1) + (M1 * c + m + 1))
                        if m == 0:
                            pe.wait_ge(dense_landed, r * 32 + 16 * (c + 1))
                        op = pe.matmul(bank[m][:], wt1_dense[0:DENSE, m * P:(m + 1) * P], dense_t[0:DENSE, :],
                                       start=True, stop=False)
                        if m == M1 - 1:
                            op.then_inc(dense_used, 1)
                    for kb in range(KB):
                        last = three_passes(bank[m][:], (hi[:, kb, cols], lo[:, kb, cols]),
                                            (x_hi[:, cb, kb, :], x_lo[:, cb, kb, :]), False,
                                            source == AND and kb == KB - 1)
                    if source == AND:
                        last.then_inc(h1_done, 1)

                def chunk(r, c):
                    for tile in range(TILES):
                        turn(r, c, REMAINING, tile)
                    for source in range(SOURCES):
                        for m in range(M1):
                            multiply(r, c, source, m)
                            if source + 1 < SOURCES:
                                turn(r, c, source + 1, m)
                    for kb in range(M1):
                        pe.wait_ge(h1_out, r * (2 * M1) + (4 + M1 * c + kb + 1))
                        for m in range(M2):
                            last = pe.matmul(bank[6 + m][:], wt2[:, kb, m * P:(m + 1) * P], top_ring[:, kb % 3, :],
                                             start=(kb == 0), stop=(kb == M1 - 1))
                            if kb == M1 - 1:
                                last.then_inc(h2_done, 1)
                            elif kb == 0 and m == M2 - 1:
                                last.then_inc(h1_used, 1)
                    for m in range(M2):
                        pe.wait_ge(h2_out, r * (2 * M2) + (M2 * c + m + 1))
                        last = pe.matmul(bank[6][0:1, :], columns[:, COL_WT3 + m:COL_WT3 + m + 1], top_ring[:, 1 + m, :],
                                         start=(m == 0), stop=(m == M2 - 1))
                    last.then_inc(y_done, 1)
                repeat(pe, 0, CHUNKS, chunk)


def general_path(nc, picks_i, remaining, inv_count, t):
    def blocked(first):
        w = t["w_blocks"][first * KB:(first + 1) * KB].rearrange("b p k c -> k p b c")
        return [w[kb] for kb in range(KB)]

    def plain(w):
        return [w[r:min(r + P, w.shape[0]), :] for r in range(0, w.shape[0], P)]

    not_layers = [("not1", blocked(2), H), ("not2", blocked(3), H)]
    layers = (not_layers * len(NOTS)
              + [("and", blocked(4) + blocked(5), H)] * (len(ANDS) // 2)
              + [("or", blocked(0) + blocked(1), H)] * (len(ORS) // 2)
              + [("and2", plain(t["Wa2"]), H), ("or2", plain(t["Wo2"]), H),
                 ("top1", plain(t["W_top1"]), N1),
                 ("top2", [t["wt2"][:, kb, :] for kb in range(M1)], N2),
                 ("top3", plain(t["W_top3"]), 1)])
    LAYERS = len(layers)
    WRING = 3
    WBLOCKS = sum(len(w) for _, w, _ in layers)
    assert WBLOCKS % WRING == 0
    blocks_until = [sum(len(w) for _, w, _ in layers[:n + 1]) for n in range(LAYERS)]
    COPIES = LAYERS + 1
    NTILES = BATCH // P
    DVE_STEPS = 42

    with ExitStack() as ctx:
        sb = lambda name, shape, dt=F32: ctx.enter_context(nc.sbuf_tensor(name, shape, dt))
        sem = lambda name: ctx.enter_context(nc.semaphore(name))
        iv = sb("iv", [P, FIELDS, H])
        g_ids = sb("g_ids", [P, NTILES, FIELDS], I32)
        g_ids_now = sb("g_ids_now", [P, FIELDS], I32)
        rows = sb("rows", [P, 2, H])
        rows_t = sb("rows_t", [P, 2 * KB, P])
        weights = sb("weights", [P, WRING, H])
        sum_t = sb("sum_t", [P, H])
        tanh_rows = sb("tanh_rows", [P, 2, H])
        u_sum = sb("u_sum", [P, 2, H])
        bias = {name: sb("row_" + name, [P, t[name].shape[0]]) for name in ("bn1", "bn2", "ba1", "bo1", "ba2", "bo2", "b_top1", "b_top2")}
        dense_sb = sb("dense_sb", [P, DENSE])
        g_identity = sb("g_identity", [P, P])
        y_rows = sb("y_rows", [P, 1])
        turned_ps = ctx.enter_context(nc.psum_tensor("turned_ps", [P, 2 * KB * P], F32))
        out_ps = ctx.enter_context(nc.psum_tensor("out_ps", [P, H], F32))

        g_consts = sem("g_consts")
        g_identity_ready = sem("g_identity_ready")
        g_ids_ready = sem("g_ids_ready")
        lookups_begun = sem("lookups_begun")
        gathered = sem("gathered")
        dense_rows = sem("dense_rows")
        g_w_landed = [sem(f"g_w_landed{i}") for i in range(WRING)]
        w_used = sem("w_used")
        ready = sem("ready")
        g_turned = sem("g_turned")
        copied = sem("copied")
        tanh_input, tanh_done = sem("tanh_input"), sem("tanh_done")
        y_ready, g_y_stored = sem("y_ready"), sem("g_y_stored")
        tile_done = sem("tile_done")
        dve_step = sem("dve_step")
        picking = sem("picking")
        y_tiles = t["y_rows"].rearrange("(n p) o -> n p o", p=P)
        dense_tiles = t["dense_ctx"].rearrange("(n p) d -> n p d", p=P)

        with nc.Block() as block:

            @block.sync
            def _(sp):
                for name, tile in bias.items():
                    sp.dma_start(tile[:], t[name].partition_broadcast(P)).then_inc(g_consts, 16)
                sp.dma_start(g_ids[:], t["ids"].rearrange("p c (n f) -> p (c n) f", f=FIELDS)).then_inc(g_consts, 16)
                with sp.Fori(0, NTILES) as i:
                    sp.wait_ge(tile_done, i + 1)
                    sp.dma_start(dense_sb[:], dense_tiles[i]).then_inc(dense_rows, 16)
                    n = 0
                    for _, blocks, width in layers:
                        for w in blocks:
                            dst = weights[0:w.shape[0], n % WRING, 0:width]
                            if len(w.shape) == 3:
                                dst = dst.rearrange("p (b c) -> p b c", b=KB)
                            sp.wait_ge(w_used, i * WBLOCKS + (n + 1))
                            sp.dma_start(dst, w).then_inc(g_w_landed[n % WRING], 16)
                            n += 1
                sp.wait_ge(g_y_stored, 16 * NTILES)

            @block.gpsimd
            def _(pool):
                pool.memset(g_identity[:], 0.0).then_inc(g_identity_ready, 1)
                pool.wait_ge(g_identity_ready, 1)
                pool.affine_select(out=g_identity[:], in_=g_identity[:], compare_op=ALU.not_equal, fill=1.0,
                                   base=0, pattern=[[-1, P]], channel_multiplier=1).then_inc(g_identity_ready, 1)
                pool.wait_ge(g_consts, 16 * (len(bias) + 1))
                with pool.Fori(0, NTILES) as i:
                    pool.wait_ge(tile_done, i + 1)
                    pool.tensor_copy(g_ids_now[:], g_ids[:, i, :]).then_inc(g_ids_ready, 1)
                    pool.wait_ge(g_ids_ready, i + 1)
                    pool.sem_inc(lookups_begun, 1)
                    for f in range(FIELDS):
                        pool.indirect_dma_start(
                            out=iv[:, f, :], out_offset=None, in_=t["tables"][f],
                            in_offset=bass.IndirectOffsetOnAxis(ap=g_ids_now[:, f:f + 1].bitcast(U32), axis=0),
                            bounds_check=VOCAB[f] - 1, oob_is_err=False).then_inc(gathered, 16)

            @block.scalar
            def _(act):
                with act.Fori(0, NTILES) as i:
                    copies = tanhs = 0
                    for n, (name, blocks, _) in enumerate(layers):
                        act.wait_ge(g_turned, i * LAYERS + (n + 1))
                        whole = len(blocks) - (name == "top1")
                        act.activation(rows_t[:, 0:whole, :], turned_ps[:, 0:whole * P].rearrange("p (k c) -> p k c", c=P),
                                       ACT.Copy).then_inc(copied, 1)
                        if name == "top1":
                            act.activation(rows_t[0:DENSE, KB, :], turned_ps[0:DENSE, KB * P:(KB + 1) * P],
                                           ACT.Copy).then_inc(copied, 1)
                        if name == "not2":
                            act.wait_ge(tanh_input, i * len(NOTS) + (tanhs + 1))
                            act.activation(tanh_rows[:, tanhs, :], sum_t[:], ACT.Tanh).then_inc(tanh_done, 1)
                            tanhs += 1
                    act.wait_ge(y_ready, i + 1)
                    act.dma_start(y_tiles[i], y_rows[:]).then_inc(g_y_stored, 16)

            @block.tensor
            def _(pe):
                pe.sem_inc(w_used, WRING)
                pe.wait_ge(g_identity_ready, 2)
                with pe.Fori(0, NTILES) as i:
                    copies = used = 0
                    flat = rows[:].rearrange("p a n -> p (a n)")
                    for n, (name, blocks, width) in enumerate(layers):
                        pe.wait_ge(ready, i * LAYERS + (n + 1))
                        for kb, w in enumerate(blocks):
                            size = w.shape[0]
                            last = pe.transpose(turned_ps[0:size, kb * P:(kb + 1) * P], flat[:, kb * P:kb * P + size],
                                                g_identity[:])
                        last.then_inc(g_turned, 1)
                        copies += 1 + (name == "top1")
                        pe.wait_ge(copied, i * COPIES + copies)
                        for kb, w in enumerate(blocks):
                            size, slot = w.shape[0], used % WRING
                            pe.wait_ge(g_w_landed[slot], i * (16 * WBLOCKS // WRING) + 16 * (used // WRING + 1))
                            for at in range(0, width, WIDE):
                                cols = slice(at, min(at + WIDE, width))
                                last = pe.matmul(out_ps[:, cols], rows_t[0:size, kb, :], weights[0:size, slot, cols],
                                                 start=(kb == 0), stop=(kb == len(blocks) - 1))
                            last.then_inc(w_used, 1)
                            used += 1

            @block.vector
            def _(dve):
                field = [dve.value_load(picks_i[0:1, e:e + 1], min_val=0, max_val=FIELDS - 1) for e in range(len(STRUCTURE))]
                dve.sem_inc(tile_done, 1)
                dve.wait_ge(g_consts, 16 * (len(bias) + 1))
                with dve.Fori(0, NTILES) as i:
                    steps = [0]

                    def did(op):
                        steps[0] += 1
                        op.then_inc(dve_step, 1)
                        dve.wait_ge(dve_step, i * DVE_STEPS + steps[0])

                    def of_field(e):
                        return iv[:, bass.ds(field[e], 1), :].rearrange("p a n -> p (a n)")

                    def add_bias(name, width=H):
                        did(dve.tensor_tensor(sum_t[:, 0:width], out_ps[:, 0:width], bias[name][:], ALU.add))

                    def rectify(to, width=H):
                        did(dve.tensor_scalar(to, sum_t[:, 0:width], 0.0, None, ALU.max))

                    dve.wait_ge(gathered, i * (16 * FIELDS) + 16 * FIELDS)
                    nots = pairs = 0
                    for n, (name, blocks, _) in enumerate(layers):
                        if name in ("not1", "and", "or"):
                            dve.sem_inc(picking, 1)
                        if name == "not1":
                            did(dve.tensor_copy(rows[:, 0, :], of_field(nots)))
                        elif name in ("and", "or"):
                            if pairs == 0:
                                for s in range(len(NOTS)):
                                    did(dve.tensor_copy(of_field(s), tanh_rows[:, s, :]))
                                    dve.sem_inc(picking, 1)
                            for side in range(2):
                                did(dve.tensor_copy(rows[:, side, :], of_field(len(NOTS) + 2 * pairs + side)))
                                dve.sem_inc(picking, 1)
                        elif name == "and2":
                            did(dve.tensor_copy(rows[:, 0, :], u_sum[:, 0, :]))
                        elif name == "or2":
                            did(dve.tensor_copy(rows[:, 0, :], u_sum[:, 1, :]))
                        elif name == "top1":
                            dve.wait_ge(dense_rows, i * 16 + 16)
                            did(dve.tensor_copy(rows[:, 1, 0:DENSE], dense_sb[:]))
                        dve.sem_inc(ready, 1)
                        dve.wait_ge(w_used, i * WBLOCKS + (WRING + blocks_until[n]))
                        if name == "not1":
                            add_bias("bn1")
                            rectify(rows[:, 0, :])
                        elif name == "not2":
                            add_bias("bn2")
                            dve.sem_inc(tanh_input, 1)
                            dve.wait_ge(tanh_done, i * len(NOTS) + (nots + 1))
                            nots += 1
                        elif name in ("and", "or"):
                            add_bias("ba1" if name == "and" else "bo1")
                            total = u_sum[:, 0 if name == "and" else 1, :]
                            if pairs in (0, len(ANDS) // 2):
                                rectify(total)
                            else:
                                did(dve.scalar_tensor_tensor(out=total, in0=sum_t[:], scalar=0.0, in1=total,
                                                             op0=ALU.max, op1=ALU.add))
                            pairs += 1
                        elif name == "and2":
                            did(dve.scalar_tensor_tensor(out=u_sum[:, 0, :], in0=bias["ba2"][:], scalar=float(len(ANDS) // 2),
                                                         in1=out_ps[:], op0=ALU.mult, op1=ALU.add))
                        elif name == "or2":
                            did(dve.scalar_tensor_tensor(out=sum_t[:], in0=bias["bo2"][:], scalar=float(len(ORS) // 2),
                                                         in1=out_ps[:], op0=ALU.mult, op1=ALU.add))
                            did(dve.tensor_tensor(sum_t[:], sum_t[:], u_sum[:, 0, :], ALU.add))
                            for f in range(FIELDS):
                                did(dve.scalar_tensor_tensor(out=sum_t[:], in0=iv[:, f, :], scalar=remaining[:, f:f + 1],
                                                             in1=sum_t[:], op0=ALU.mult, op1=ALU.add))
                            did(dve.tensor_scalar(rows[:, 0, :], sum_t[:], inv_count[:, 0:1], None, ALU.mult))
                        elif name == "top1":
                            add_bias("b_top1", N1)
                            rectify(rows[:, 0, 0:N1], N1)
                        elif name == "top2":
                            add_bias("b_top2", N2)
                            rectify(rows[:, 0, 0:N2], N2)
                        else:
                            did(dve.tensor_copy(y_rows[:], out_ps[:, 0:1]))
                            dve.sem_inc(y_ready, 1)
                            dve.wait_ge(g_y_stored, i * 16 + 16)
                    dve.sem_inc(tile_done, 1)
                    assert steps[0] == DVE_STEPS, steps[0]


def build(nc, t):
    with ExitStack() as ctx:
        picks_i, flag, remaining, inv_count = read_structure(nc, ctx, t["not_idx"], t["and_pairs"], t["or_pairs"])
        other = nc.values_load(flag[0:1, 0:1], min_val=0, max_val=1,
                               skip_runtime_bounds_check_because="a comparison's result is 0 or 1")
        with nc.If(other == 0):
            table_path(nc, inv_count, t)
        with nc.Else():
            general_path(nc, picks_i, remaining, inv_count, t)


def _pieces(np, table):
    n = -(-table.shape[0] // COLS)
    full = np.zeros((n * COLS, H), table.dtype)
    full[:table.shape[0]] = table
    return full.reshape(n, COLS, KB, P).transpose(0, 3, 2, 1)


def _blocks(np, w):
    return w.reshape(KB, P, w.shape[1] // P, P).transpose(2, 1, 0, 3)


def _columns(v):
    return v.reshape(-1, P).T


def kernel(**inputs):
    import numpy as np
    import concourse.bacc as _bacc
    from concourse import mybir as _mybir
    from concourse.bass_utils import run_bass_kernel_spmd as _run

    a = {k: np.asarray(v) for k, v in inputs.items()}
    L = {k[len("L0_rec_"):]: v for k, v in a.items() if k.startswith("L0_rec_")}
    wa, wo = L["Wa1"], L["Wo1"]
    arrays = {
        "x_pieces": np.concatenate([_pieces(np, a[f"tbl_{f}"]) for f in FIELD_ORDER]
                                   + [_pieces(np, L["Wa2"]), _pieces(np, L["Wo2"])]),
        "w_blocks": np.concatenate([_blocks(np, w) for w in (wo[:H], wo[H:], L["Wn1"], L["Wn2"], wa[:H], wa[H:],
                                                            a["W_top1"][:H])]),
        "columns": np.concatenate([_columns(v) for v in (L["bn1"], L["bn2"], L["ba2"], L["bo2"], a["b_top1"],
                                                         a["b_top2"], a["W_top3"][:, 0])], axis=1),
        "wt2": a["W_top2"].reshape(M1, P, N2).transpose(1, 0, 2),
        "dense_t": a["dense_ctx"].reshape(CHUNKS, CHUNK, DENSE).transpose(0, 2, 1),
        "ids": a["ids"].reshape(CHUNKS, TILES, P, FIELDS).transpose(2, 0, 1, 3).reshape(P, CHUNKS, TILES * FIELDS),
        "W_top1": a["W_top1"], "bo1": L["bo1"], "ba1": L["ba1"],
        "not_idx": L["not_idx"], "and_pairs": L["and_pairs"], "or_pairs": L["or_pairs"],
    }
    for name in ("bn1", "bn2", "ba2", "bo2", "Wa2", "Wo2"):
        arrays[name] = L[name]
    for name in ["b_top1", "b_top2", "W_top3", "dense_ctx"] + [f"tbl_{f}" for f in range(FIELDS)]:
        arrays[name] = a[name]
    arrays = {k: np.ascontiguousarray(v) for k, v in arrays.items()}
    nc = _bacc.Bacc("TRN2", target_bir_lowering=False, num_devices=1)
    t = {k: nc.dram_tensor(k + "_in", v.shape, _mybir.dt.from_np(v.dtype), kind="ExternalInput").ap()
         for k, v in arrays.items()}
    t["tables"] = [t[f"tbl_{f}"] for f in range(FIELDS)]
    y = nc.dram_tensor("y_out", (BATCH, 1), F32, kind="ExternalOutput").ap()
    t["y_rows"] = y
    t["y"] = y.rearrange("(c n) o -> c o n", n=CHUNK)
    build(nc, t)
    r = _run(nc, [{k + "_in": v for k, v in arrays.items()}], core_ids=[0])
    return r.results[0]["y_out"]
```

```python
from contextlib import ExitStack

import concourse.bass as bass
from concourse import mybir

F32 = mybir.dt.float32
F32R = mybir.dt.float32r
I32 = mybir.dt.int32
U32 = mybir.dt.uint32
ALU = mybir.AluOpType
ACT = mybir.ActivationFunctionType
AX = mybir.AxisListType

P = 128
H = 1024
KB = H // P
N1, N2 = 512, 256
M1, M2 = N1 // P, N2 // P
BATCH = 2048
FIELDS = 8
DENSE = 16
VOCAB = [1250, 1000, 1250, 1250, 1250, 1250, 1250, 12500]
NOTS, ANDS, ORS = [2, 3], [0, 1, 2, 3], [4, 5]
STRUCTURE = NOTS + ANDS + ORS
PAIRS = (len(ANDS) + len(ORS)) // 2

COLS = 256
WIDE = 512
FIELD_ORDER = [4, 5, 2, 3, 0, 1]
PIECES = {f: -(-VOCAB[f] // COLS) for f in FIELD_ORDER}
FIRST_PIECE, _at = {}, 0
for _f in FIELD_ORDER:
    FIRST_PIECE[_f] = _at
    _at += PIECES[_f]
FIRST_PIECE["Wa2"] = _at
FIRST_PIECE["Wo2"] = _at + H // COLS
TOTAL_PIECES = _at + 2 * (H // COLS)

CHUNK = 512
CHUNKS = BATCH // CHUNK
TILES = CHUNK // P
SOURCES = 3

COL_BN1, COL_BN2, COL_BA2, COL_BO2 = 0, KB, 2 * KB, 3 * KB
COL_BT1 = 4 * KB
COL_BT2 = COL_BT1 + M1
COL_WT3 = COL_BT2 + M2
NCOLS = COL_WT3 + M2


def repeat(engine, first, count, body, period=2):
    rounds = count // period
    done = 0
    if rounds >= 2:
        with engine.Fori(0, rounds) as r:
            for s in range(period):
                body(r, first + s)
        done = rounds * period
    for i in range(first + done, first + count):
        body(0, i)


class Segment:

    def __init__(self, kind, weights, source, piece, units, target, bias=None, func=None):
        self.kind = kind
        self.weights = weights
        self.source, self.piece = source, piece
        self.units, self.target, self.bias, self.func = units, target, bias, func
        self.pieces_per_unit = 2 if kind == "columns" else 1
        self.groups_per_unit = {"rows": 4, "columns": 8, "fold": 2}[kind]

    def place(self, unit, group, piece):
        self.unit0, self.group0, self.piece0 = unit, group, piece
        self.unit_end = unit + self.units
        self.group_end = group + self.units * self.groups_per_unit
        self.pieces = self.units * self.pieces_per_unit
        self.piece_end = piece + self.pieces
        return self.unit_end, self.group_end, self.piece_end


class FirstLoads:

    def __init__(self, nc, ctx, t):
        sem = lambda name: ctx.enter_context(nc.semaphore(name))
        self.stage = ctx.enter_context(nc.sbuf_tensor("stage", [P, 4 * 2 * H], F32))
        self.x_raw = self.stage[:, 0:2 * KB * COLS].rearrange("p (s k c) -> p s k c", s=2, k=KB)
        self.w_raw = self.stage[:, 2 * KB * COLS:2 * KB * COLS + 3 * H].rearrange("p (s k c) -> p s k c", s=3, k=KB)
        self.x_landed = [sem(f"x_landed{i}") for i in range(2)]
        self.w_landed = [sem(f"w_landed{i}") for i in range(3)]
        self.x_src, self.w_src = t["x_pieces"], t["w_blocks"]

    def start(self, sp):
        for k in range(3):
            sp.dma_start(self.w_raw[:, k], self.w_src[k]).then_inc(self.w_landed[k], 16)
            if k < 2:
                sp.dma_start(self.x_raw[:, k], self.x_src[FIRST_PIECE[FIELD_ORDER[0]] + k]).then_inc(self.x_landed[k], 16)

    def wait(self, sp):
        for landed in self.x_landed + self.w_landed:
            sp.wait_ge(landed, 16)


def read_structure(nc, ctx, not_idx, and_pairs, or_pairs, first_loads):
    keep = lambda name, shape, dt: ctx.enter_context(nc.sbuf_tensor(name, shape, dt))
    flag = keep("flag", [P, 1], I32)
    picks_i = keep("picks_i", [P, len(STRUCTURE)], I32)
    remaining = keep("remaining", [P, FIELDS], F32)
    inv_count = keep("inv_count", [P, 1], F32)
    with ExitStack() as inner:
        _read_structure(nc, inner, not_idx, and_pairs, or_pairs, picks_i, flag, remaining, inv_count, first_loads)
    return picks_i, flag, remaining, inv_count


def _read_structure(nc, ctx, not_idx, and_pairs, or_pairs, picks_i, flag, remaining, inv_count, first_loads):
    sb = lambda name, shape, dt: ctx.enter_context(nc.sbuf_tensor(name, shape, dt))
    n, npair = len(STRUCTURE), len(ANDS) + len(ORS)
    picks = sb("picks", [P, n], F32)
    expected = sb("expected", [P, n], F32)
    field_no = sb("field_no", [P, FIELDS], F32)
    differ = sb("differ", [P, n], F32)
    differ_any = sb("differ_any", [P, 1], F32)
    hits = sb("hits", [P, npair, FIELDS], F32)
    processed = sb("processed", [P, FIELDS], F32)
    count = sb("count", [P, 1], F32)
    count_all = sb("count_all", [P, 1], F32)
    picks_landed = ctx.enter_context(nc.semaphore("picks_landed"))
    step = ctx.enter_context(nc.semaphore("structure_step"))

    with nc.Block() as block:

        @block.sync
        def _(sp):
            sp.dma_start(picks_i[:, 0:2], not_idx.partition_broadcast(P)).then_inc(picks_landed, 16)
            sp.dma_start(picks_i[:, 2:6], and_pairs.rearrange("a b -> (a b)").partition_broadcast(P)).then_inc(picks_landed, 16)
            sp.dma_start(picks_i[:, 6:8], or_pairs.rearrange("a b -> (a b)").partition_broadcast(P)).then_inc(picks_landed, 16)
            first_loads.start(sp)

        @block.vector
        def _(dve):
            for i, v in enumerate(STRUCTURE):
                dve.memset(expected[:, i:i + 1], float(v)).then_inc(step, 1)
            for f in range(FIELDS):
                dve.memset(field_no[:, f:f + 1], float(f)).then_inc(step, 1)
            at = n + FIELDS
            dve.wait_ge(picks_landed, 48)
            dve.tensor_copy(picks[:], picks_i[:]).then_inc(step, 1)
            dve.wait_ge(step, at + 1)
            dve.tensor_tensor(differ[:], picks[:], expected[:], ALU.not_equal).then_inc(step, 1)
            for e in range(npair):
                dve.tensor_scalar(hits[:, e, :], field_no[:], picks[:, 2 + e:3 + e], None,
                                  ALU.is_equal).then_inc(step, 1)
            dve.wait_ge(step, at + 2 + npair)
            dve.tensor_reduce(differ_any[:], differ[:], AX.X, ALU.max).then_inc(step, 1)
            dve.tensor_reduce(processed[:], hits[:].rearrange("p e f -> p f e"), AX.X,
                              ALU.max).then_inc(step, 1)
            dve.wait_ge(step, at + 4 + npair)
            dve.tensor_copy(flag[:], differ_any[:]).then_inc(step, 1)
            dve.tensor_scalar(remaining[:], processed[:], -1.0, 1.0, ALU.mult, ALU.add).then_inc(step, 1)
            dve.wait_ge(step, at + 6 + npair)
            dve.tensor_reduce(count[:], remaining[:], AX.X, ALU.add).then_inc(step, 1)
            dve.wait_ge(step, at + 7 + npair)
            dve.tensor_scalar(count_all[:], count[:], float(PAIRS), None, ALU.add).then_inc(step, 1)
            dve.wait_ge(step, at + 8 + npair)
            dve.reciprocal(inv_count[:], count_all[:]).then_inc(step, 1)
            dve.wait_ge(step, at + 9 + npair)


def table_path(nc, inv_count, first_loads, t):
    with ExitStack() as ctx:
        sb = lambda name, shape, dt=F32: ctx.enter_context(nc.sbuf_tensor(name, shape, dt))
        sem = lambda name: ctx.enter_context(nc.semaphore(name))
        dram = lambda name, shape: nc.dram_tensor(name, shape, F32, kind="Internal").ap()

        hidden_t = dram("hidden_t", [2 * PIECES[2], P, KB, COLS])
        tanh_t = dram("tanh_t", [2 * PIECES[2], P, KB, COLS])
        half = {f: dram(f"half_{f}", [PIECES[f] * COLS, H]) for f in FIELD_ORDER}

        w_hi, w_lo = sb("w_hi", [P, KB, H], F32R), sb("w_lo", [P, KB, H], F32R)
        z_hi, z_lo = sb("z_hi", [P, KB, N1], F32R), sb("z_lo", [P, KB, N1], F32R)
        x_hi = sb("x_hi", [P, 2, KB, WIDE], F32R)
        x_lo = sb("x_lo", [P, 2, KB, WIDE], F32R)
        b2_parts = sb("b2_parts", [P, KB, 2], F32R)
        stage, x_raw, w_raw = first_loads.stage, first_loads.x_raw, first_loads.w_raw
        bias_row = stage[:, 7 * H:8 * H]
        looked = stage[:, :].rearrange("p (s two n) -> p s two n", s=4, two=2)
        small = sb("small", [P, 7, WIDE])
        out_ring = small[:, 0:4, :]
        top_ring = small[:, 0:3, :]
        wt2 = small[:, 3:5, :].rearrange("p a b -> p (a b)").rearrange("p (k n) -> p k n", k=M1)
        wt1_dense = small[:, 5, :]
        dense_t = small[:, 6, :]
        identity = sb("identity", [P, P])
        columns = sb("columns", [P, NCOLS])
        b2 = sb("b2", [P, KB])
        bias1 = sb("bias1", [P, M1])
        ids = sb("ids", [P, CHUNKS, TILES * FIELDS], I32)
        ids_now = sb("ids_now", [P, 2, TILES * FIELDS], I32)

        bank = [ctx.enter_context(nc.psum_tensor(f"bank{i}", [P, WIDE], F32)) for i in range(8)]

        x_src = t["x_pieces"]
        segments = [
            Segment("rows", 0, x_src, FIRST_PIECE[4], PIECES[4], half[4], bias="bo1"),
            Segment("rows", 1, x_src, FIRST_PIECE[5], PIECES[5], half[5]),
            Segment("columns", 2, x_src, FIRST_PIECE[2], PIECES[2], hidden_t, func=(ACT.Relu, COL_BN1)),
            Segment("columns", 3, hidden_t, 0, PIECES[2], tanh_t, func=(ACT.Tanh, COL_BN2)),
            Segment("rows", 4, x_src, FIRST_PIECE[0], PIECES[0], half[0], bias="ba1"),
            Segment("rows", 4, tanh_t, 0, PIECES[2], half[2], bias="ba1"),
            Segment("rows", 5, tanh_t, PIECES[2], PIECES[3], half[3]),
            Segment("rows", 5, x_src, FIRST_PIECE[1], PIECES[1], half[1]),
            Segment("fold", 6, x_src, FIRST_PIECE["Wa2"], H // COLS, 0),
            Segment("fold", 6, x_src, FIRST_PIECE["Wo2"], H // COLS, 1),
        ]
        u = g = q = 0
        for s in segments:
            u, g, q = s.place(u, g, q)
        UNITS, GROUPS, ALL_PIECES = u, g, q
        STORED_GROUPS = segments[7].group_end
        made_by = {id(hidden_t): segments[2], id(tanh_t): segments[3]}
        last_of = {s.weights: s for s in segments}
        first_of = {s.weights: s for s in reversed(segments)}
        BLOCKS = [KB] * 6 + [M1]
        block0 = [sum(BLOCKS[:i]) for i in range(len(BLOCKS) + 1)]
        TOP = len(BLOCKS) - 1
        BIASED = {}
        n = 0
        for i, s in enumerate(segments):
            BIASED[i] = n
            if s.bias:
                n += s.units * s.groups_per_unit
        BIASED_ALL = n
        first_and = [s.bias for s in segments].index("ba1")

        x_landed, w_landed = first_loads.x_landed, first_loads.w_landed
        x_rounded = sem("x_rounded")
        x_split = sem("x_split")
        w_scaled = sem("w_scaled")
        w_rounded = sem("w_rounded")
        w_split = sem("w_split")
        products = sem("products")
        bank_free = sem("bank_free")
        fold_rounded = sem("fold_rounded")
        fold_split = sem("fold_split")
        bias_landed = sem("bias_landed")
        biased = sem("biased")
        stored = [sem(f"stored{i}") for i in range(4)]
        consts_landed = sem("consts_landed")
        identity_ready = sem("identity_ready")
        b2_step = sem("b2_step")
        b2_product = sem("b2_product")
        top_landed = sem("top_landed")
        dense_landed = sem("dense_landed")
        dense_used = sem("dense_used")
        ids_ready = sem("ids_ready")
        looked_up = [sem(f"looked_up{i}") for i in range(4)]
        slot_taken = sem("slot_taken")
        added = sem("added")
        first_added = sem("first_added")
        relued = sem("relued")
        summed = sem("summed")
        and_summed = sem("and_summed")
        turned = sem("turned")
        turned_hi = sem("turned_hi")
        turned_lo = sem("turned_lo")
        h1_done, h1_out = sem("h1_done"), sem("h1_out")
        h1_used = sem("h1_used")
        h2_done, h2_out = sem("h2_done"), sem("h2_out")
        y_done, y_out = sem("y_done"), sem("y_out")
        y_stored = sem("y_stored")
        y_free = sem("y_free")

        C_UNIT = UNITS % 2
        PER_CHUNK = SOURCES * TILES * 2
        REMAINING, OR, AND = range(SOURCES)

        batch_steps = [("turn", 0, REMAINING, tile) for tile in range(TILES)]
        for c in range(CHUNKS):
            for source in range(SOURCES):
                for m in range(M1):
                    batch_steps.append(("multiply", c, source, m))
                    if source < AND:
                        batch_steps.append(("turn", c, source + 1, m))
                    elif c + 1 < CHUNKS:
                        batch_steps.append(("turn", c + 1, REMAINING, m))
                    if source == AND and m:
                        batch_steps.append(("top2", c, m - 1))
                    if source == REMAINING and c and m == 0:
                        batch_steps.append(("top2", c - 1, M1 - 1))
                    if source == REMAINING and c and m == 2:
                        batch_steps.append(("top3", c - 1))
        batch_steps += [("top2", CHUNKS - 1, M1 - 1), ("top3", CHUNKS - 1)]
        turns = [tuple(at) for name, *at in batch_steps if name == "turn"]
        next_turn = dict(zip(turns, turns[1:]))

        def rows_of(dst):
            return dst.rearrange("(n p) c -> n p c", p=P)

        def weight_parts(w, b):
            hi, lo = (z_hi, z_lo) if w == TOP else (w_hi, w_lo)
            cols = slice(b * P, (b + 1) * P)
            return w_raw[:, (block0[w] + b) % 3], hi[:, :, cols], lo[:, :, cols]

        def weights_lo(engine, w, b):
            raw, hi, lo = weight_parts(w, b)
            engine.tensor_tensor(lo, raw, hi, ALU.subtract).then_inc(w_split, 1)

        with nc.Block() as block:

            @block.sync
            def _(sp):
                def load_weights(w, blocks):
                    for b in blocks:
                        n = block0[w] + b
                        if n >= 3:
                            sp.wait_ge(w_split, n - 2)
                        sp.dma_start(w_raw[:, n % 3], t["w_blocks"][n]).then_inc(w_landed[n % 3], 16)

                def load_piece(s, r, k):
                    q = s.piece0 + k
                    if not (isinstance(r, int) and q < 2):
                        sp.wait_ge(x_split, r * 2 + (q - 1))
                    made = made_by.get(id(s.source))
                    if made is not None:
                        unit = (s.piece + k) // 2
                        for ring in range(4):
                            sp.wait_ge(stored[ring], r * (16 * 2) + 16 * (made.group0 + 8 * (unit + 1)) // 4)
                    sp.dma_start(x_raw[:, q % 2], s.source[r * 2 + (s.piece + k)]).then_inc(x_landed[q % 2], 16)

                sp.sem_inc(y_free, 1)
                load_weights(0, range(3, BLOCKS[0]))
                for i, s in enumerate(segments):
                    w = s.weights
                    if first_of[w] is s and w + 1 < len(BLOCKS):
                        load_weights(w + 1, range(0, 3))
                    repeat(sp, 2, s.pieces - 2, lambda r, k: load_piece(s, r, k))
                    if i + 1 < len(segments):
                        for k in range(2):
                            load_piece(segments[i + 1], 0, k)
                    if last_of[w] is s and w + 1 < len(BLOCKS):
                        load_weights(w + 1, range(3, BLOCKS[w + 1]))
                sp.wait_ge(stored[3], 16 * STORED_GROUPS // 4)
                sp.dma_start(wt2, t["wt2"]).then_inc(top_landed, 16)
                sp.dma_start(wt1_dense[0:DENSE, :], t["W_top1"][H:H + DENSE, :]).then_inc(top_landed, 16)

                def load_dense(c):
                    sp.wait_ge(dense_used, c + 1)
                    sp.dma_start(dense_t[0:DENSE, :], t["dense_t"][c]).then_inc(dense_landed, 16)

                load_dense(0)
                for c in range(CHUNKS):
                    if c + 1 < CHUNKS:
                        load_dense(c + 1)
                    sp.wait_ge(y_out, c + 1)
                    sp.dma_start(t["y"][c], top_ring[0:1, 0, :]).then_inc(y_stored, 16)
                    sp.wait_ge(y_stored, 16 * (c + 1))
                    sp.sem_inc(y_free, 1)
                sp.wait_ge(y_stored, 16 * CHUNKS)

            @block.gpsimd
            def _(pool):
                pool.memset(identity[:], 0.0).then_inc(identity_ready, 1)
                pool.wait_ge(identity_ready, 1)
                pool.affine_select(out=identity[:], in_=identity[:], compare_op=ALU.not_equal, fill=1.0,
                                   base=0, pattern=[[-1, P]], channel_multiplier=1).then_inc(identity_ready, 1)
                for w, blocks in enumerate(BLOCKS):
                    for b in range(blocks if w else 0):
                        n = block0[w] + b
                        if w == TOP:
                            pool.wait_ge(w_landed[n % 3], 16 * (n // 3 + 1))
                            pool.tensor_scalar(w_raw[:, n % 3], w_raw[:, n % 3], inv_count[:, 0:1], None,
                                               ALU.mult).then_inc(w_scaled, 1)
                        pool.wait_ge(w_rounded, n + 1)
                        weights_lo(pool, w, b)

                pool.wait_ge(w_split, block0[-1])
                pool.wait_ge(x_split, ALL_PIECES)
                pool.wait_ge(biased, BIASED_ALL)
                pool.wait_ge(consts_landed, 16 * 2)
                for ring in range(4):
                    pool.wait_ge(stored[ring], 16 * STORED_GROUPS // 4)

                def lookup(slot, c, tile, fields):
                    pool.sem_inc(slot_taken, 1)
                    for j, f in enumerate(fields):
                        index = ids_now[:, c % 2, tile * FIELDS + f:tile * FIELDS + f + 1]
                        src = t["tables"][f] if f >= 6 else half[f]
                        pool.indirect_dma_start(
                            out=looked[:, slot, j, :], out_offset=None, in_=src,
                            in_offset=bass.IndirectOffsetOnAxis(ap=index.bitcast(U32), axis=0),
                            bounds_check=src.shape[0] - 1, oob_is_err=False,
                        ).then_inc(looked_up[slot], 16)

                def chunk(r, c):
                    pool.tensor_copy(ids_now[:, c % 2, :], ids[:, r * 2 + c, :]).then_inc(ids_ready, 1)
                    pool.wait_ge(ids_ready, r * 2 + (c + 1))
                    base = PER_CHUNK * (c + 1)
                    turned_at = lambda source, tile: r * (2 * PER_CHUNK) + (base + source * TILES * 2 + 2 * (tile + 1))
                    for tile in range(TILES):
                        if tile % 2 == 0:
                            pool.wait_ge(turned, r * (2 * PER_CHUNK) + (base - PER_CHUNK + AND * TILES * 2 + 2 * (2 + tile // 2 + 1)))
                        else:
                            pool.wait_ge(and_summed, r * 8 + 4 * c + (2 + tile // 2 + 1))
                        lookup(tile, c, tile, (6, 7))
                    for tile in range(TILES):
                        pool.wait_ge(turned, turned_at(REMAINING, tile))
                        lookup(tile, c, tile, (4, 5))
                    for tile in range(TILES):
                        for second, fields in enumerate(((0, 1), (2, 3))):
                            slot = (2 * tile + second) % 4
                            if tile < 2:
                                pool.wait_ge(turned, turned_at(OR, slot))
                            elif second:
                                pool.wait_ge(and_summed, r * 8 + 4 * (c + 1) + (tile - 2 + 1))
                            else:
                                pool.wait_ge(turned, turned_at(AND, tile - 2))
                            lookup(slot, c, tile, fields)
                repeat(pool, 0, CHUNKS, chunk)

            @block.scalar
            def _(act):
                act.dma_start(columns[:], t["columns"]).then_inc(consts_landed, 16)
                act.dma_start(ids[:], t["ids"]).then_inc(consts_landed, 16)
                act.dma_start(bias_row, t["bo1"].partition_broadcast(P)).then_inc(bias_landed, 16)
                act.sem_inc(bank_free, 4)
                act.sem_inc(h1_out, 4)
                act.wait_ge(consts_landed, 32)

                def evacuate(s, i, r, k, j):
                    per = s.groups_per_unit
                    g = s.group0 + k * per + j
                    ring = g % 4
                    act.wait_ge(products, r * (2 * per) + (g + 1))
                    if not (isinstance(r, int) and g < 4):
                        act.wait_ge(stored[ring], r * (16 * 2 * per // 4) + 16 * (g // 4))
                    if s.kind == "columns":
                        func, col = s.func
                        act.activation(out_ring[:, ring, :], bank[ring][:], func,
                                       bias=columns[:, col + j:col + j + 1]).then_inc(bank_free, 1)
                        dst = s.target.rearrange("(u a) p m c -> u m p a c", a=2)[r * 2 + k, j]
                        src = out_ring[:, ring, :].rearrange("p (a c) -> p a c", a=2)
                    else:
                        act.activation(out_ring[:, ring, :], bank[ring][:], ACT.Copy).then_inc(bank_free, 1)
                        side, tile = j // 2, j % 2
                        dst = rows_of(s.target)[r * 4 + (2 * k + tile), :, side * WIDE:(side + 1) * WIDE]
                        src = out_ring[:, ring, :]
                    if s.bias:
                        act.wait_ge(biased, r * (2 * per) + (BIASED[i] + k * per + j + 1))
                    else:
                        act.wait_ge(bank_free, r * (2 * per) + (4 + g + 1))
                    act.dma_start(dst, src).then_inc(stored[ring], 16)

                def weights_hi(w, b):
                    n = block0[w] + b
                    raw, hi, _ = weight_parts(w, b)
                    if w == TOP:
                        act.wait_ge(w_scaled, b + 1)
                    else:
                        act.wait_ge(w_landed[n % 3], 16 * (n // 3 + 1))
                    act.activation(hi, raw, ACT.Copy).then_inc(w_rounded, 1)

                def next_weights(s, j):
                    w = s.weights + 1
                    if s.kind == "columns":
                        blocks = [j]
                    elif j % 2 == 0:
                        blocks = []
                    else:
                        blocks = range((j // 2) * KB // 2, (j // 2 + 1) * KB // 2)
                    for b in blocks:
                        if b < BLOCKS[w]:
                            weights_hi(w, b)

                def fold(s, r, k, j):
                    g = s.group0 + k * 2 + j
                    act.wait_ge(products, r * 4 + (g + 1))
                    act.activation(w_hi[:, 2 * k + j, s.target * N1:(s.target + 1) * N1], bank[g % 4][:],
                                   ACT.Copy).then_inc(fold_rounded, 1)
                    act.wait_ge(fold_split, g - segments[8].group0 + 1)
                    act.sem_inc(bank_free, 1)

                for b in range(BLOCKS[0]):
                    weights_hi(0, b)
                for i, s in enumerate(segments):
                    if s.kind == "fold":
                        for k in range(s.units):
                            for j in range(2):
                                fold(s, 0, k, j)
                        continue
                    if i == first_and:
                        act.wait_ge(biased, BIASED[i])
                        act.dma_start(bias_row, t["ba1"].partition_broadcast(P)).then_inc(bias_landed, 16)
                    per = s.groups_per_unit
                    unit = lambda r, k: [evacuate(s, i, r, k, j) for j in range(per)]
                    last = s is last_of[s.weights]
                    first = 1 if i == 0 else 0
                    if first:
                        unit(0, 0)
                    repeat(act, first, s.units - last - first, unit)
                    if last:
                        for j in range(per):
                            evacuate(s, i, 0, s.units - 1, j)
                            next_weights(s, j)

                for ring in range(4):
                    act.wait_ge(stored[ring], 16 * STORED_GROUPS // 4)

                def turn_hi(c, source, tile):
                    func = ACT.Relu if source == OR else ACT.Copy
                    cb = (C_UNIT + SOURCES * c + source) % 2
                    for h in range(2):
                        n = PER_CHUNK * c + (source * TILES + tile) * 2 + h
                        act.wait_ge(turned, PER_CHUNK + n + 1)
                        act.activation(x_hi[:, cb, 4 * h:4 * h + 4, tile * P:(tile + 1) * P],
                                       bank[4 + h][:].rearrange("p (b c) -> p b c", b=4), func).then_inc(turned_hi, 1)

                def relu_second(c, tile):
                    slot = (2 * tile + 1) % 4
                    act.wait_ge(added, 4 * c + tile + 1)
                    act.activation(looked[:, slot, 0, :], looked[:, slot, 0, :], ACT.Relu).then_inc(relued, 1)

                def h1_block(c, m):
                    act.wait_ge(h1_done, M1 * c + m + 1)
                    if m == 0:
                        act.wait_ge(b2_step, 5)
                        act.wait_ge(y_free, c + 1)
                    if m == 3:
                        act.wait_ge(h1_used, c + 1)
                    act.activation(top_ring[:, m % 3, :], bank[m][:], ACT.Relu,
                                   bias=bias1[:, m:m + 1]).then_inc(h1_out, 1)

                def h2_blocks(c):
                    for m in range(M2):
                        act.wait_ge(h2_done, M2 * c + m + 1)
                        act.activation(top_ring[:, 1 + m, :], bank[6 + m][:], ACT.Relu,
                                       bias=columns[:, COL_BT2 + m:COL_BT2 + m + 1]).then_inc(h2_out, 1)

                def y_row(c):
                    act.wait_ge(y_done, c + 1)
                    act.activation(top_ring[0:1, 0, :], bank[6][0:1, :], ACT.Copy).then_inc(y_out, 1)

                for name, *at in batch_steps:
                    if name == "turn":
                        following = next_turn.get(tuple(at))
                        if following and following[1] == AND:
                            relu_second(following[0], following[2])
                        turn_hi(*at)
                    elif name == "multiply" and at[1] == AND:
                        h1_block(at[0], at[2])
                    elif name == "top2" and at[1] == M1 - 1:
                        h2_blocks(at[0])
                    elif name == "top3":
                        y_row(at[0])

            @block.vector
            def _(dve):
                dve.sem_inc(and_summed, 4)
                dve.sem_inc(turned_lo, 2)

                def split(s, r, k):
                    u = s.unit0 + k
                    buffer = u % 2
                    if not (isinstance(r, int) and u < 2):
                        per = s.groups_per_unit
                        if k >= 2:
                            dve.wait_ge(products, r * (2 * per) + (s.group0 + (k - 1) * per))
                        else:
                            before = segments[segments.index(s) - 1]
                            dve.wait_ge(products, before.group_end - (1 - k) * before.groups_per_unit)
                    for a in range(s.pieces_per_unit):
                        q = s.piece0 + k * s.pieces_per_unit + a
                        step = 2 * s.pieces_per_unit
                        cols = slice(a * COLS, (a + 1) * COLS)
                        dve.wait_ge(x_landed[q % 2], r * (16 * step // 2) + 16 * (q // 2 + 1))
                        dve.tensor_copy(x_hi[:, buffer, :, cols], x_raw[:, q % 2]).then_inc(x_rounded, 1)
                        dve.wait_ge(x_rounded, r * step + (q + 1))
                        dve.tensor_tensor(x_lo[:, buffer, :, cols], x_raw[:, q % 2], x_hi[:, buffer, :, cols],
                                          ALU.subtract).then_inc(x_split, 1)

                def add_bias(s, i, r, k):
                    for j in range(4):
                        g = s.group0 + k * 4 + j
                        side = j // 2
                        dve.wait_ge(bank_free, r * 8 + (4 + g + 1))
                        tile = out_ring[:, g % 4, :]
                        dve.tensor_tensor(tile, tile, bias_row[:, side * WIDE:(side + 1) * WIDE],
                                          ALU.add).then_inc(biased, 1)

                def fold_lo(s, k):
                    for j in range(2):
                        g = s.group0 + k * 2 + j
                        cols = slice(s.target * N1, (s.target + 1) * N1)
                        dve.wait_ge(fold_rounded, g - segments[8].group0 + 1)
                        dve.tensor_tensor(w_lo[:, 2 * k + j, cols], bank[g % 4][:], w_hi[:, 2 * k + j, cols],
                                          ALU.subtract).then_inc(fold_split, 1)

                for k in range(2):
                    split(segments[0], 0, k)
                    for b in range(k * KB // 2, (k + 1) * KB // 2):
                        dve.wait_ge(w_rounded, b + 1)
                        weights_lo(dve, 0, b)
                for i, s in enumerate(segments):
                    if s.bias:
                        dve.wait_ge(bias_landed, 16 if s.bias == "bo1" else 32)

                    def own(r, k):
                        if s.bias:
                            add_bias(s, i, r, k)
                        elif s.kind == "fold":
                            fold_lo(s, k)

                    def step(r, k):
                        own(r, k)
                        split(s, r, k + 2)
                    if s.kind == "fold":
                        for k in range(s.units - 2):
                            step(0, k)
                    else:
                        repeat(dve, 0, s.units - 2, step)
                    for k in range(2):
                        own(0, s.units - 2 + k)
                        if i + 1 < len(segments):
                            split(segments[i + 1], 0, k)

                dve.scalar_tensor_tensor(out=b2[:], in0=columns[:, COL_BA2:COL_BA2 + KB], scalar=float(len(ANDS) // 2),
                                         in1=columns[:, COL_BO2:COL_BO2 + KB], op0=ALU.mult, op1=ALU.add).then_inc(b2_step, 1)
                dve.wait_ge(b2_step, 1)
                dve.tensor_copy(b2_parts[:, :, 0], b2[:]).then_inc(b2_step, 1)
                dve.wait_ge(b2_step, 2)
                dve.tensor_tensor(b2_parts[:, :, 1], b2[:], b2_parts[:, :, 0], ALU.subtract).then_inc(b2_step, 1)
                dve.wait_ge(b2_product, 1)
                dve.tensor_reduce(bias1[:], bank[7][:, 0:2 * M1].rearrange("p (m two) -> p m two", two=2),
                                  AX.X, ALU.add).then_inc(b2_step, 1)
                dve.wait_ge(b2_step, 4)
                dve.tensor_tensor(bias1[:], bias1[:], columns[:, COL_BT1:COL_BT1 + M1], ALU.add).then_inc(b2_step, 1)

                def add_rows(c, source, tile):
                    if source != AND:
                        slots = [tile]
                        use = c * 4 + source
                    else:
                        slots = [(2 * tile + 1) % 4, (2 * tile) % 4]
                        use = c * 4 + 2 + tile // 2
                    for n, slot in enumerate(slots):
                        dve.wait_ge(looked_up[slot], 32 * (use + 1))
                        a, b = looked[:, slot, 0, :], looked[:, slot, 1, :]
                        op = dve.tensor_tensor(a, a, b, ALU.add)
                        if source != AND:
                            op.then_inc(summed, 1)
                        elif n == 0:
                            op.then_inc(added, 1)
                        else:
                            op.then_inc(first_added, 1)
                            dve.wait_ge(first_added, 4 * c + tile + 1)
                            dve.wait_ge(relued, 4 * c + tile + 1)
                            dve.scalar_tensor_tensor(out=a, in0=a, scalar=0.0, in1=looked[:, slots[0], 0, :],
                                                     op0=ALU.max, op1=ALU.add).then_inc(and_summed, 1)

                def turn_lo(c, source, tile):
                    cb = (C_UNIT + SOURCES * c + source) % 2
                    for h in range(2):
                        n = PER_CHUNK * c + (source * TILES + tile) * 2 + h
                        where = (slice(None), cb, slice(4 * h, 4 * h + 4), slice(tile * P, (tile + 1) * P))
                        turned_bank = bank[4 + h][:].rearrange("p (b c) -> p b c", b=4)
                        dve.wait_ge(turned_hi, n + 1)
                        if source == OR:
                            dve.scalar_tensor_tensor(out=x_lo[where], in0=turned_bank, scalar=0.0, in1=x_hi[where],
                                                     op0=ALU.max, op1=ALU.subtract).then_inc(turned_lo, 1)
                        else:
                            dve.tensor_tensor(x_lo[where], turned_bank, x_hi[where], ALU.subtract).then_inc(turned_lo, 1)

                add_rows(0, REMAINING, 0)
                for name, *at in batch_steps:
                    if name == "turn":
                        following = next_turn.get(tuple(at))
                        if following:
                            add_rows(*following)
                        turn_lo(*at)

            @block.tensor
            def _(pe):
                pe.sem_inc(turned, PER_CHUNK)
                pe.sem_inc(dense_used, 1)

                def three_passes(out, stationary, moving, start, stop):
                    (s_hi, s_lo), (m_hi, m_lo) = stationary, moving
                    pe.matmul(out, s_hi, m_hi, start=start, stop=False)
                    pe.matmul(out, s_hi, m_lo, start=False, stop=False)
                    return pe.matmul(out, s_lo, m_hi, start=False, stop=stop)

                def unit(s, r, k):
                    per = s.groups_per_unit
                    buffer = (s.unit0 + k) % 2
                    pe.wait_ge(x_split, r * (2 * s.pieces_per_unit) + (s.piece0 + (k + 1) * s.pieces_per_unit))
                    for j in range(per):
                        g = s.group0 + k * per + j
                        pe.wait_ge(bank_free, r * (2 * per) + (g + 1))
                        if s.kind == "columns":
                            pe.wait_ge(w_split, block0[s.weights] + j + 1)
                        elif j == 0:
                            pe.wait_ge(w_split, block0[s.weights] + (KB // 2 if s.kind == "rows" else M1))
                        elif j == 2:
                            pe.wait_ge(w_split, block0[s.weights] + KB)
                        for kb in range(KB):
                            if s.kind == "columns":
                                cols = slice(j * P, (j + 1) * P)
                                stationary = w_hi[:, kb, cols], w_lo[:, kb, cols]
                                moving = x_hi[:, buffer, kb, :], x_lo[:, buffer, kb, :]
                            else:
                                side, tile = (j // 2, j % 2) if s.kind == "rows" else (0, j)
                                rows = slice(tile * P, (tile + 1) * P)
                                cols = slice(side * WIDE, (side + 1) * WIDE)
                                stationary = x_hi[:, buffer, kb, rows], x_lo[:, buffer, kb, rows]
                                moving = (w_hi[:, kb, cols], w_lo[:, kb, cols]) if s.kind == "rows" else (z_hi[:, kb, :], z_lo[:, kb, :])
                            last = three_passes(bank[g % 4][:], stationary, moving, kb == 0, kb == KB - 1)
                        last.then_inc(products, 1)

                for s in segments:
                    repeat(pe, 0, s.units, lambda r, k: unit(s, r, k))

                pe.wait_ge(b2_step, 3)
                for m in range(M1):
                    for kb in range(KB):
                        for part, z in enumerate((z_hi, z_lo)):
                            last = pe.matmul(bank[7][:, 2 * m:2 * m + 2], z[:, kb, m * P:(m + 1) * P], b2_parts[:, kb, :],
                                             start=(kb == 0 and part == 0), stop=(kb == KB - 1 and part == 1))
                last.then_inc(b2_product, 1)
                pe.wait_ge(bank_free, 4 + GROUPS)
                pe.wait_ge(identity_ready, 2)
                pe.wait_ge(top_landed, 32)
                pe.wait_ge(b2_step, 4)

                def turn(c, source, tile):
                    if source == AND:
                        pe.wait_ge(and_summed, 4 * c + 4 + tile + 1)
                        slot = (2 * tile) % 4
                    else:
                        pe.wait_ge(summed, c * 2 * TILES + source * TILES + tile + 1)
                        slot = tile
                    for h in range(2):
                        n = PER_CHUNK * c + (source * TILES + tile) * 2 + h
                        pe.wait_ge(turned_lo, n + 1)
                        for b in range(4):
                            kb = 4 * h + b
                            last = pe.transpose(bank[4 + h][:, b * P:(b + 1) * P],
                                                looked[:, slot, 0, kb * P:(kb + 1) * P], identity[:])
                        last.then_inc(turned, 1)

                def multiply(c, source, m):
                    cb = (C_UNIT + SOURCES * c + source) % 2
                    hi, lo, at = [(z_hi, z_lo, 0), (w_hi, w_lo, N1), (w_hi, w_lo, 0)][source]
                    cols = slice(at + m * P, at + (m + 1) * P)
                    if m == 0:
                        pe.wait_ge(turned_lo, 2 + PER_CHUNK * c + (source + 1) * TILES * 2)
                    if source == REMAINING:
                        pe.wait_ge(h1_out, M1 * c + m + 1)
                        if m == 0:
                            pe.wait_ge(dense_landed, 16 * (c + 1))
                        op = pe.matmul(bank[m][:], wt1_dense[0:DENSE, m * P:(m + 1) * P], dense_t[0:DENSE, :],
                                       start=True, stop=False)
                        if m == M1 - 1:
                            op.then_inc(dense_used, 1)
                    for kb in range(KB):
                        last = three_passes(bank[m][:], (hi[:, kb, cols], lo[:, kb, cols]),
                                            (x_hi[:, cb, kb, :], x_lo[:, cb, kb, :]), False,
                                            source == AND and kb == KB - 1)
                    if source == AND:
                        last.then_inc(h1_done, 1)

                def top2(c, kb):
                    pe.wait_ge(h1_out, 4 + M1 * c + kb + 1)
                    if kb == 0 and c:
                        pe.wait_ge(y_out, c)
                    for m in range(M2):
                        last = pe.matmul(bank[6 + m][:], wt2[:, kb, m * P:(m + 1) * P], top_ring[:, kb % 3, :],
                                         start=(kb == 0), stop=(kb == M1 - 1))
                        if kb == M1 - 1:
                            last.then_inc(h2_done, 1)
                        elif kb == 0 and m == M2 - 1:
                            last.then_inc(h1_used, 1)

                def top3(c):
                    for m in range(M2):
                        pe.wait_ge(h2_out, M2 * c + m + 1)
                        last = pe.matmul(bank[6][0:1, :], columns[:, COL_WT3 + m:COL_WT3 + m + 1], top_ring[:, 1 + m, :],
                                         start=(m == 0), stop=(m == M2 - 1))
                    last.then_inc(y_done, 1)

                do = {"turn": turn, "multiply": multiply, "top2": top2, "top3": top3}
                for name, *at in batch_steps:
                    do[name](*at)


def general_path(nc, picks_i, remaining, inv_count, first_loads, t):
    def blocked(first):
        w = t["w_blocks"][first * KB:(first + 1) * KB].rearrange("b p k c -> k p b c")
        return [w[kb] for kb in range(KB)]

    def plain(w):
        return [w[r:min(r + P, w.shape[0]), :] for r in range(0, w.shape[0], P)]

    not_layers = [("not1", blocked(2), H), ("not2", blocked(3), H)]
    layers = (not_layers * len(NOTS)
              + [("and", blocked(4) + blocked(5), H)] * (len(ANDS) // 2)
              + [("or", blocked(0) + blocked(1), H)] * (len(ORS) // 2)
              + [("and2", plain(t["Wa2"]), H), ("or2", plain(t["Wo2"]), H),
                 ("top1", plain(t["W_top1"]), N1),
                 ("top2", [t["wt2"][:, kb, :] for kb in range(M1)], N2),
                 ("top3", plain(t["W_top3"]), 1)])
    LAYERS = len(layers)
    WRING = 3
    WBLOCKS = sum(len(w) for _, w, _ in layers)
    assert WBLOCKS % WRING == 0
    blocks_until = [sum(len(w) for _, w, _ in layers[:n + 1]) for n in range(LAYERS)]
    COPIES = LAYERS + 1
    NTILES = BATCH // P
    DVE_STEPS = 42

    with ExitStack() as ctx:
        sb = lambda name, shape, dt=F32: ctx.enter_context(nc.sbuf_tensor(name, shape, dt))
        sem = lambda name: ctx.enter_context(nc.semaphore(name))
        iv = sb("iv", [P, FIELDS, H])
        g_ids = sb("g_ids", [P, NTILES, FIELDS], I32)
        g_ids_now = sb("g_ids_now", [P, FIELDS], I32)
        rows = sb("rows", [P, 2, H])
        rows_t = sb("rows_t", [P, 2 * KB, P])
        weights = sb("weights", [P, WRING, H])
        sum_t = sb("sum_t", [P, H])
        tanh_rows = sb("tanh_rows", [P, 2, H])
        u_sum = sb("u_sum", [P, 2, H])
        bias = {name: sb("row_" + name, [P, t[name].shape[0]]) for name in ("bn1", "bn2", "ba1", "bo1", "ba2", "bo2", "b_top1", "b_top2")}
        dense_sb = sb("dense_sb", [P, DENSE])
        g_identity = sb("g_identity", [P, P])
        y_rows = sb("y_rows", [P, 1])
        turned_ps = ctx.enter_context(nc.psum_tensor("turned_ps", [P, 2 * KB * P], F32))
        out_ps = ctx.enter_context(nc.psum_tensor("out_ps", [P, H], F32))

        g_consts = sem("g_consts")
        g_identity_ready = sem("g_identity_ready")
        g_ids_ready = sem("g_ids_ready")
        lookups_begun = sem("lookups_begun")
        gathered = sem("gathered")
        dense_rows = sem("dense_rows")
        g_w_landed = [sem(f"g_w_landed{i}") for i in range(WRING)]
        w_used = sem("w_used")
        ready = sem("ready")
        g_turned = sem("g_turned")
        copied = sem("copied")
        tanh_input, tanh_done = sem("tanh_input"), sem("tanh_done")
        y_ready, g_y_stored = sem("y_ready"), sem("g_y_stored")
        tile_done = sem("tile_done")
        dve_step = sem("dve_step")
        picking = sem("picking")
        y_tiles = t["y_rows"].rearrange("(n p) o -> n p o", p=P)
        dense_tiles = t["dense_ctx"].rearrange("(n p) d -> n p d", p=P)

        with nc.Block() as block:

            @block.sync
            def _(sp):
                first_loads.wait(sp)
                for name, tile in bias.items():
                    sp.dma_start(tile[:], t[name].partition_broadcast(P)).then_inc(g_consts, 16)
                sp.dma_start(g_ids[:], t["ids"].rearrange("p c (n f) -> p (c n) f", f=FIELDS)).then_inc(g_consts, 16)
                with sp.Fori(0, NTILES) as i:
                    sp.wait_ge(tile_done, i + 1)
                    sp.dma_start(dense_sb[:], dense_tiles[i]).then_inc(dense_rows, 16)
                    n = 0
                    for _, blocks, width in layers:
                        for w in blocks:
                            dst = weights[0:w.shape[0], n % WRING, 0:width]
                            if len(w.shape) == 3:
                                dst = dst.rearrange("p (b c) -> p b c", b=KB)
                            sp.wait_ge(w_used, i * WBLOCKS + (n + 1))
                            sp.dma_start(dst, w).then_inc(g_w_landed[n % WRING], 16)
                            n += 1
                sp.wait_ge(g_y_stored, 16 * NTILES)

            @block.gpsimd
            def _(pool):
                pool.memset(g_identity[:], 0.0).then_inc(g_identity_ready, 1)
                pool.wait_ge(g_identity_ready, 1)
                pool.affine_select(out=g_identity[:], in_=g_identity[:], compare_op=ALU.not_equal, fill=1.0,
                                   base=0, pattern=[[-1, P]], channel_multiplier=1).then_inc(g_identity_ready, 1)
                pool.wait_ge(g_consts, 16 * (len(bias) + 1))
                with pool.Fori(0, NTILES) as i:
                    pool.wait_ge(tile_done, i + 1)
                    pool.tensor_copy(g_ids_now[:], g_ids[:, i, :]).then_inc(g_ids_ready, 1)
                    pool.wait_ge(g_ids_ready, i + 1)
                    pool.sem_inc(lookups_begun, 1)
                    for f in range(FIELDS):
                        pool.indirect_dma_start(
                            out=iv[:, f, :], out_offset=None, in_=t["tables"][f],
                            in_offset=bass.IndirectOffsetOnAxis(ap=g_ids_now[:, f:f + 1].bitcast(U32), axis=0),
                            bounds_check=VOCAB[f] - 1, oob_is_err=False).then_inc(gathered, 16)

            @block.scalar
            def _(act):
                with act.Fori(0, NTILES) as i:
                    copies = tanhs = 0
                    for n, (name, blocks, _) in enumerate(layers):
                        act.wait_ge(g_turned, i * LAYERS + (n + 1))
                        whole = len(blocks) - (name == "top1")
                        act.activation(rows_t[:, 0:whole, :], turned_ps[:, 0:whole * P].rearrange("p (k c) -> p k c", c=P),
                                       ACT.Copy).then_inc(copied, 1)
                        if name == "top1":
                            act.activation(rows_t[0:DENSE, KB, :], turned_ps[0:DENSE, KB * P:(KB + 1) * P],
                                           ACT.Copy).then_inc(copied, 1)
                        if name == "not2":
                            act.wait_ge(tanh_input, i * len(NOTS) + (tanhs + 1))
                            act.activation(tanh_rows[:, tanhs, :], sum_t[:], ACT.Tanh).then_inc(tanh_done, 1)
                            tanhs += 1
                    act.wait_ge(y_ready, i + 1)
                    act.dma_start(y_tiles[i], y_rows[:]).then_inc(g_y_stored, 16)

            @block.tensor
            def _(pe):
                pe.sem_inc(w_used, WRING)
                pe.wait_ge(g_identity_ready, 2)
                with pe.Fori(0, NTILES) as i:
                    copies = used = 0
                    flat = rows[:].rearrange("p a n -> p (a n)")
                    for n, (name, blocks, width) in enumerate(layers):
                        pe.wait_ge(ready, i * LAYERS + (n + 1))
                        for kb, w in enumerate(blocks):
                            size = w.shape[0]
                            last = pe.transpose(turned_ps[0:size, kb * P:(kb + 1) * P], flat[:, kb * P:kb * P + size],
                                                g_identity[:])
                        last.then_inc(g_turned, 1)
                        copies += 1 + (name == "top1")
                        pe.wait_ge(copied, i * COPIES + copies)
                        for kb, w in enumerate(blocks):
                            size, slot = w.shape[0], used % WRING
                            pe.wait_ge(g_w_landed[slot], i * (16 * WBLOCKS // WRING) + 16 * (used // WRING + 1))
                            for at in range(0, width, WIDE):
                                cols = slice(at, min(at + WIDE, width))
                                last = pe.matmul(out_ps[:, cols], rows_t[0:size, kb, :], weights[0:size, slot, cols],
                                                 start=(kb == 0), stop=(kb == len(blocks) - 1))
                            last.then_inc(w_used, 1)
                            used += 1

            @block.vector
            def _(dve):
                field = [dve.value_load(picks_i[0:1, e:e + 1], min_val=0, max_val=FIELDS - 1) for e in range(len(STRUCTURE))]
                dve.sem_inc(tile_done, 1)
                dve.wait_ge(g_consts, 16 * (len(bias) + 1))
                with dve.Fori(0, NTILES) as i:
                    steps = [0]

                    def did(op):
                        steps[0] += 1
                        op.then_inc(dve_step, 1)
                        dve.wait_ge(dve_step, i * DVE_STEPS + steps[0])

                    def of_field(e):
                        return iv[:, bass.ds(field[e], 1), :].rearrange("p a n -> p (a n)")

                    def add_bias(name, width=H):
                        did(dve.tensor_tensor(sum_t[:, 0:width], out_ps[:, 0:width], bias[name][:], ALU.add))

                    def rectify(to, width=H):
                        did(dve.tensor_scalar(to, sum_t[:, 0:width], 0.0, None, ALU.max))

                    dve.wait_ge(gathered, i * (16 * FIELDS) + 16 * FIELDS)
                    nots = pairs = 0
                    for n, (name, blocks, _) in enumerate(layers):
                        if name in ("not1", "and", "or"):
                            dve.sem_inc(picking, 1)
                        if name == "not1":
                            did(dve.tensor_copy(rows[:, 0, :], of_field(nots)))
                        elif name in ("and", "or"):
                            if pairs == 0:
                                for s in range(len(NOTS)):
                                    did(dve.tensor_copy(of_field(s), tanh_rows[:, s, :]))
                                    dve.sem_inc(picking, 1)
                            for side in range(2):
                                did(dve.tensor_copy(rows[:, side, :], of_field(len(NOTS) + 2 * pairs + side)))
                                dve.sem_inc(picking, 1)
                        elif name == "and2":
                            did(dve.tensor_copy(rows[:, 0, :], u_sum[:, 0, :]))
                        elif name == "or2":
                            did(dve.tensor_copy(rows[:, 0, :], u_sum[:, 1, :]))
                        elif name == "top1":
                            dve.wait_ge(dense_rows, i * 16 + 16)
                            did(dve.tensor_copy(rows[:, 1, 0:DENSE], dense_sb[:]))
                        dve.sem_inc(ready, 1)
                        dve.wait_ge(w_used, i * WBLOCKS + (WRING + blocks_until[n]))
                        if name == "not1":
                            add_bias("bn1")
                            rectify(rows[:, 0, :])
                        elif name == "not2":
                            add_bias("bn2")
                            dve.sem_inc(tanh_input, 1)
                            dve.wait_ge(tanh_done, i * len(NOTS) + (nots + 1))
                            nots += 1
                        elif name in ("and", "or"):
                            add_bias("ba1" if name == "and" else "bo1")
                            total = u_sum[:, 0 if name == "and" else 1, :]
                            if pairs in (0, len(ANDS) // 2):
                                rectify(total)
                            else:
                                did(dve.scalar_tensor_tensor(out=total, in0=sum_t[:], scalar=0.0, in1=total,
                                                             op0=ALU.max, op1=ALU.add))
                            pairs += 1
                        elif name == "and2":
                            did(dve.scalar_tensor_tensor(out=u_sum[:, 0, :], in0=bias["ba2"][:], scalar=float(len(ANDS) // 2),
                                                         in1=out_ps[:], op0=ALU.mult, op1=ALU.add))
                        elif name == "or2":
                            did(dve.scalar_tensor_tensor(out=sum_t[:], in0=bias["bo2"][:], scalar=float(len(ORS) // 2),
                                                         in1=out_ps[:], op0=ALU.mult, op1=ALU.add))
                            did(dve.tensor_tensor(sum_t[:], sum_t[:], u_sum[:, 0, :], ALU.add))
                            for f in range(FIELDS):
                                did(dve.scalar_tensor_tensor(out=sum_t[:], in0=iv[:, f, :], scalar=remaining[:, f:f + 1],
                                                             in1=sum_t[:], op0=ALU.mult, op1=ALU.add))
                            did(dve.tensor_scalar(rows[:, 0, :], sum_t[:], inv_count[:, 0:1], None, ALU.mult))
                        elif name == "top1":
                            add_bias("b_top1", N1)
                            rectify(rows[:, 0, 0:N1], N1)
                        elif name == "top2":
                            add_bias("b_top2", N2)
                            rectify(rows[:, 0, 0:N2], N2)
                        else:
                            did(dve.tensor_copy(y_rows[:], out_ps[:, 0:1]))
                            dve.sem_inc(y_ready, 1)
                            dve.wait_ge(g_y_stored, i * 16 + 16)
                    dve.sem_inc(tile_done, 1)
                    assert steps[0] == DVE_STEPS, steps[0]


def build(nc, t):
    with ExitStack() as ctx:
        first_loads = FirstLoads(nc, ctx, t)
        picks_i, flag, remaining, inv_count = read_structure(nc, ctx, t["not_idx"], t["and_pairs"], t["or_pairs"], first_loads)
        other = nc.values_load(flag[0:1, 0:1], min_val=0, max_val=1,
                               skip_runtime_bounds_check_because="a comparison's result is 0 or 1")
        with nc.If(other == 0):
            table_path(nc, inv_count, first_loads, t)
        with nc.Else():
            general_path(nc, picks_i, remaining, inv_count, first_loads, t)


def _pieces(np, table):
    n = -(-table.shape[0] // COLS)
    full = np.zeros((n * COLS, H), table.dtype)
    full[:table.shape[0]] = table
    return full.reshape(n, COLS, KB, P).transpose(0, 3, 2, 1)


def _blocks(np, w):
    return w.reshape(KB, P, w.shape[1] // P, P).transpose(2, 1, 0, 3)


def _columns(v):
    return v.reshape(-1, P).T


def kernel(**inputs):
    import numpy as np
    import concourse.bacc as _bacc
    from concourse import mybir as _mybir
    from concourse.bass_utils import run_bass_kernel_spmd as _run

    a = {k: np.asarray(v) for k, v in inputs.items()}
    L = {k[len("L0_rec_"):]: v for k, v in a.items() if k.startswith("L0_rec_")}
    wa, wo = L["Wa1"], L["Wo1"]
    arrays = {
        "x_pieces": np.concatenate([_pieces(np, a[f"tbl_{f}"]) for f in FIELD_ORDER]
                                   + [_pieces(np, L["Wa2"]), _pieces(np, L["Wo2"])]),
        "w_blocks": np.concatenate([_blocks(np, w) for w in (wo[:H], wo[H:], L["Wn1"], L["Wn2"], wa[:H], wa[H:],
                                                            a["W_top1"][:H])]),
        "columns": np.concatenate([_columns(v) for v in (L["bn1"], L["bn2"], L["ba2"], L["bo2"], a["b_top1"],
                                                         a["b_top2"], a["W_top3"][:, 0])], axis=1),
        "wt2": a["W_top2"].reshape(M1, P, N2).transpose(1, 0, 2),
        "dense_t": a["dense_ctx"].reshape(CHUNKS, CHUNK, DENSE).transpose(0, 2, 1),
        "ids": a["ids"].reshape(CHUNKS, TILES, P, FIELDS).transpose(2, 0, 1, 3).reshape(P, CHUNKS, TILES * FIELDS),
        "W_top1": a["W_top1"], "bo1": L["bo1"], "ba1": L["ba1"],
        "not_idx": L["not_idx"], "and_pairs": L["and_pairs"], "or_pairs": L["or_pairs"],
    }
    for name in ("bn1", "bn2", "ba2", "bo2", "Wa2", "Wo2"):
        arrays[name] = L[name]
    for name in ["b_top1", "b_top2", "W_top3", "dense_ctx"] + [f"tbl_{f}" for f in range(FIELDS)]:
        arrays[name] = a[name]
    arrays = {k: np.ascontiguousarray(v) for k, v in arrays.items()}
    nc = _bacc.Bacc("TRN2", target_bir_lowering=False, num_devices=1)
    t = {k: nc.dram_tensor(k + "_in", v.shape, _mybir.dt.from_np(v.dtype), kind="ExternalInput").ap()
         for k, v in arrays.items()}
    t["tables"] = [t[f"tbl_{f}"] for f in range(FIELDS)]
    y = nc.dram_tensor("y_out", (BATCH, 1), F32, kind="ExternalOutput").ap()
    t["y_rows"] = y
    t["y"] = y.rearrange("(c n) o -> c o n", n=CHUNK)
    build(nc, t)
    r = _run(nc, [{k + "_in": v for k, v in arrays.items()}], core_ids=[0])
    return r.results[0]["y_out"]
```

```python
from contextlib import ExitStack

import concourse.bass as bass
from concourse import mybir

F32 = mybir.dt.float32
F32R = mybir.dt.float32r
I32 = mybir.dt.int32
U32 = mybir.dt.uint32
ALU = mybir.AluOpType
ACT = mybir.ActivationFunctionType
AX = mybir.AxisListType

P = 128
H = 1024
KB = H // P
N1, N2 = 512, 256
M1, M2 = N1 // P, N2 // P
BATCH = 2048
FIELDS = 8
DENSE = 16
VOCAB = [1250, 1000, 1250, 1250, 1250, 1250, 1250, 12500]
NOTS, ANDS, ORS = [2, 3], [0, 1, 2, 3], [4, 5]
STRUCTURE = NOTS + ANDS + ORS
PAIRS = (len(ANDS) + len(ORS)) // 2
REMAINING_FIELDS = [f for f in range(8) if f not in ANDS + ORS]
SUMMANDS = PAIRS + len(REMAINING_FIELDS)

COLS = 250
FOLD_COLS = 2 * P
WIDE = 512
FIELD_ORDER = [2, 3, 4, 5, 0, 1]
PIECES = {f: VOCAB[f] // COLS for f in FIELD_ORDER}
assert all(VOCAB[f] % COLS == 0 for f in FIELD_ORDER)
FIRST_PIECE, _at = {}, 0
for _f in FIELD_ORDER:
    FIRST_PIECE[_f] = _at
    _at += PIECES[_f]

CHUNK = 512
CHUNKS = BATCH // CHUNK
TILES = CHUNK // P
SOURCES = 3

COL_BN1, COL_BN2, COL_BA2, COL_BO2 = 0, KB, 2 * KB, 3 * KB
COL_BT1 = 4 * KB
COL_BT2 = COL_BT1 + M1
COL_WT3 = COL_BT2 + M2
NCOLS = COL_WT3 + M2


def repeat(engine, first, count, body, period=2):
    rounds = count // period
    done = 0
    if rounds >= 2:
        with engine.Fori(0, rounds) as r:
            for s in range(period):
                body(r, first + s)
        done = rounds * period
    for i in range(first + done, first + count):
        body(0, i)


class Segment:

    def __init__(self, kind, weights, source, piece, units, target, bias=None, func=None):
        self.kind = kind
        self.weights = weights
        self.source, self.piece = source, piece
        self.units, self.target, self.bias, self.func = units, target, bias, func
        self.cols = FOLD_COLS if kind == "fold" else COLS
        self.tile = self.cols // 2
        self.pieces_per_unit = 2 if kind == "columns" else 1
        self.groups_per_unit = {"rows": 4, "columns": 8, "fold": 2}[kind]

    def place(self, unit, group, piece):
        self.unit0, self.group0, self.piece0 = unit, group, piece
        self.unit_end = unit + self.units
        self.group_end = group + self.units * self.groups_per_unit
        self.pieces = self.units * self.pieces_per_unit
        self.piece_end = piece + self.pieces
        return self.unit_end, self.group_end, self.piece_end


class FirstLoads:

    def __init__(self, nc, ctx, t):
        sem = lambda name: ctx.enter_context(nc.semaphore(name))
        self.stage = ctx.enter_context(nc.sbuf_tensor("stage", [P, 4 * 2 * H], F32))
        self.w_raw = self.stage[:, 0:3 * H].rearrange("p (s k c) -> p s k c", s=3, k=KB)
        self.x_slots = self.stage[:, 4 * H:].rearrange("p (s n) -> p s n", s=2)
        self.x_landed = [sem(f"x_landed{i}") for i in range(2)]
        self.w_landed = [sem(f"w_landed{i}") for i in range(3)]
        self.x_src, self.w_src = t["x_pieces"], t["w_blocks"]

    def x_raw(self, slot, cols=COLS):
        return self.x_slots[:, slot, 0:KB * cols].rearrange("p (k c) -> p k c", k=KB)

    def start(self, sp):
        for k in range(3):
            if k < 2:
                sp.dma_start(self.x_raw(k), self.x_src[k]).then_inc(self.x_landed[k], 16)
            if k != 1:
                sp.dma_start(self.w_raw[:, k // 2], self.w_src[k // 2]).then_inc(self.w_landed[k // 2], 16)
        sp.dma_start(self.w_raw[:, 2], self.w_src[2]).then_inc(self.w_landed[2], 16)

    def wait(self, sp):
        for landed in self.x_landed + self.w_landed:
            sp.wait_ge(landed, 16)


def read_structure(nc, ctx, not_idx, and_pairs, or_pairs, first_loads):
    n = len(STRUCTURE)
    keep = lambda name, shape, dt: ctx.enter_context(nc.sbuf_tensor(name, shape, dt))
    flag = keep("flag", [P, 1], I32)
    picks_i = keep("picks_i", [P, n], I32)
    picks = keep("picks", [P, n], F32)
    with ExitStack() as inner:
        sb = lambda name, shape, dt: inner.enter_context(nc.sbuf_tensor(name, shape, dt))
        expected = sb("expected", [P, n], F32)
        differ = sb("differ", [P, n], F32)
        differ_any = sb("differ_any", [P, 1], F32)
        picks_landed = inner.enter_context(nc.semaphore("picks_landed"))
        step = inner.enter_context(nc.semaphore("structure_step"))

        with nc.Block() as block:

            @block.sync
            def _(sp):
                sp.dma_start(picks_i[:, 0:2], not_idx.partition_broadcast(P)).then_inc(picks_landed, 16)
                sp.dma_start(picks_i[:, 2:6], and_pairs.rearrange("a b -> (a b)").partition_broadcast(P)).then_inc(picks_landed, 16)
                sp.dma_start(picks_i[:, 6:8], or_pairs.rearrange("a b -> (a b)").partition_broadcast(P)).then_inc(picks_landed, 16)
                first_loads.start(sp)

            @block.vector
            def _(dve):
                for i, v in enumerate(STRUCTURE):
                    dve.memset(expected[:, i:i + 1], float(v)).then_inc(step, 1)
                dve.wait_ge(picks_landed, 48)
                dve.tensor_copy(picks[:], picks_i[:]).then_inc(step, 1)
                dve.wait_ge(step, n + 1)
                dve.tensor_tensor(differ[:], picks[:], expected[:], ALU.not_equal).then_inc(step, 1)
                dve.wait_ge(step, n + 2)
                dve.tensor_reduce(differ_any[:], differ[:], AX.X, ALU.max).then_inc(step, 1)
                dve.wait_ge(step, n + 3)
                dve.tensor_copy(flag[:], differ_any[:]).then_inc(step, 1)
                dve.wait_ge(step, n + 4)
    return picks_i, picks, flag


def table_path(nc, first_loads, t):
    with ExitStack() as ctx:
        sb = lambda name, shape, dt=F32: ctx.enter_context(nc.sbuf_tensor(name, shape, dt))
        sem = lambda name: ctx.enter_context(nc.semaphore(name))
        dram = lambda name, shape: nc.dram_tensor(name, shape, F32, kind="Internal").ap()

        hidden_t = dram("hidden_t", [2 * PIECES[2], P, KB, COLS])
        tanh_t = dram("tanh_t", [2 * PIECES[2], P, KB, COLS])
        half = {f: dram(f"half_{f}", [VOCAB[f], H]) for f in FIELD_ORDER}

        w_hi, w_lo = sb("w_hi", [P, KB, H], F32R), sb("w_lo", [P, KB, H], F32R)
        z_hi, z_lo = sb("z_hi", [P, KB, N1], F32R), sb("z_lo", [P, KB, N1], F32R)
        x_hi = sb("x_hi", [P, 2, KB, WIDE], F32R)
        x_lo = sb("x_lo", [P, 2, KB, WIDE], F32R)
        b2_parts = sb("b2_parts", [P, KB, 2], F32R)
        stage, x_raw, w_raw = first_loads.stage, first_loads.x_raw, first_loads.w_raw
        bias_row = stage[:, 3 * H:4 * H]
        looked = stage[:, :].rearrange("p (s two n) -> p s two n", s=4, two=2)
        small = sb("small", [P, 5, WIDE])
        out_ring = small[:, 0:4, :]
        top_ring = small[:, 0:2, :]
        bias_rows = small[0:2, 1, :]
        dense_raw = small[0:96, 2, :]
        wt2 = small[:, 3:5, :].rearrange("p a b -> p (a b)").rearrange("p (k n) -> p k n", k=M1)
        DENSE_BLOCKS = (0, 32, 64)
        DENSE_ROWS = DENSE_BLOCKS[-1] + DENSE
        dense_w = sb("dense_w", [96, N1], F32R)
        dense_x = sb("dense_x", [96, CHUNK], F32R)
        identity = sb("identity", [P, P])
        columns = sb("columns", [P, NCOLS])
        b2 = sb("b2", [P, KB])
        bias1 = sb("bias1", [P, M1])
        ids = sb("ids", [P, CHUNKS, TILES * FIELDS], I32)
        ids_now = sb("ids_now", [P, 2, TILES * FIELDS], I32)

        bank = [ctx.enter_context(nc.psum_tensor(f"bank{i}", [P, WIDE], F32)) for i in range(8)]

        x_src = t["x_pieces"]
        segments = [
            Segment("columns", 0, x_src, FIRST_PIECE[2], PIECES[2], hidden_t, func=(ACT.Relu, COL_BN1)),
            Segment("columns", 1, hidden_t, 0, PIECES[2], tanh_t, func=(ACT.Tanh, COL_BN2)),
            Segment("rows", 2, x_src, FIRST_PIECE[4], PIECES[4], half[4], bias="bo1"),
            Segment("rows", 3, x_src, FIRST_PIECE[5], PIECES[5], half[5]),
            Segment("rows", 4, x_src, FIRST_PIECE[0], PIECES[0], half[0], bias="ba1"),
            Segment("rows", 4, tanh_t, 0, PIECES[2], half[2], bias="ba1"),
            Segment("rows", 5, tanh_t, PIECES[2], PIECES[3], half[3]),
            Segment("rows", 5, x_src, FIRST_PIECE[1], PIECES[1], half[1]),
            Segment("fold", 6, t["fold_pieces"], 0, H // FOLD_COLS, 0),
            Segment("fold", 6, t["fold_pieces"], H // FOLD_COLS, H // FOLD_COLS, 1),
        ]
        u = g = q = 0
        for s in segments:
            u, g, q = s.place(u, g, q)
        UNITS, GROUPS, ALL_PIECES = u, g, q
        STORED_GROUPS = segments[7].group_end
        made_by = {id(hidden_t): segments[0], id(tanh_t): segments[1]}
        last_of = {s.weights: s for s in segments}
        first_of = {s.weights: s for s in reversed(segments)}
        BLOCKS = [KB] * 6 + [M1]
        block0 = [sum(BLOCKS[:i]) for i in range(len(BLOCKS) + 1)]
        TOP = len(BLOCKS) - 1
        BIASED = {}
        n = 0
        for i, s in enumerate(segments):
            BIASED[i] = n
            if s.bias:
                n += s.units * s.groups_per_unit
        BIASED_ALL = n
        first_and = [s.bias for s in segments].index("ba1")

        x_landed, w_landed = first_loads.x_landed, first_loads.w_landed
        x_rounded = sem("x_rounded")
        x_split = sem("x_split")
        w_scaled = sem("w_scaled")
        w_rounded = sem("w_rounded")
        w_split = sem("w_split")
        products = sem("products")
        bank_free = sem("bank_free")
        fold_rounded = sem("fold_rounded")
        fold_split = sem("fold_split")
        bias_landed = sem("bias_landed")
        biased = sem("biased")
        stored = [sem(f"stored{i}") for i in range(4)]
        consts_landed = sem("consts_landed")
        identity_ready = sem("identity_ready")
        b2_step = sem("b2_step")
        b2_product = sem("b2_product")
        top_landed = sem("top_landed")
        dense_landed = sem("dense_landed")
        dense_cleared = sem("dense_cleared")
        dense_rounded = sem("dense_rounded")
        dense_split = sem("dense_split")
        dense_used = sem("dense_used")
        ids_ready = sem("ids_ready")
        looked_up = [sem(f"looked_up{i}") for i in range(4)]
        slot_taken = sem("slot_taken")
        added = sem("added")
        first_added = sem("first_added")
        relued = sem("relued")
        summed = sem("summed")
        and_summed = sem("and_summed")
        turned = sem("turned")
        turned_hi = sem("turned_hi")
        turned_lo = sem("turned_lo")
        h1_done, h1_out = sem("h1_done"), sem("h1_out")
        h1_used = sem("h1_used")
        h2_done, h2_out = sem("h2_done"), sem("h2_out")
        y_done, y_out = sem("y_done"), sem("y_out")
        y_stored = sem("y_stored")
        y_free = sem("y_free")

        C_UNIT = UNITS % 2
        PER_CHUNK = SOURCES * TILES * 2
        REMAINING, OR, AND = range(SOURCES)

        batch_steps = []
        for tile in range(TILES):
            if tile % 2 == 0:
                batch_steps.append(("fold", tile // 2))
            batch_steps.append(("turn", 0, REMAINING, tile))
        batch_steps.append(("features", 0))
        batch_steps.append(("bias_product",))
        for c in range(CHUNKS):
            for source in range(SOURCES):
                for m in range(M1):
                    if source < AND:
                        batch_steps.append(("turn", c, source + 1, m))
                    elif c + 1 < CHUNKS:
                        batch_steps.append(("turn", c + 1, REMAINING, m))
                    batch_steps.append(("multiply", c, source, m))
                    if c + 1 < CHUNKS and (source, m) == (AND, 1):
                        batch_steps.append(("features", c + 1))
                    if (c, source, m) == (0, REMAINING, 0):
                        batch_steps.append(("bias_turn",))
                    if source == AND and m:
                        batch_steps.append(("top2", c, m - 1))
                    if source == REMAINING and c and m == 0:
                        batch_steps.append(("top2", c - 1, M1 - 1))
                    if source == REMAINING and c and m == 2:
                        batch_steps.append(("top3", c - 1))
        batch_steps += [("top2", CHUNKS - 1, M1 - 1), ("top3", CHUNKS - 1)]
        turns = [tuple(at) for name, *at in batch_steps if name == "turn"]
        next_turn = dict(zip(turns, turns[1:]))

        def rows_of(dst):
            return dst.rearrange("(n p) c -> n p c", p=COLS // 2)

        def weight_parts(w, b):
            hi, lo = (z_hi, z_lo) if w == TOP else (w_hi, w_lo)
            cols = slice(b * P, (b + 1) * P)
            return w_raw[:, (block0[w] + b) % 3], hi[:, :, cols], lo[:, :, cols]

        def blocks_after(s, j):
            if s.kind == "columns":
                return [j]
            return range((j // 2) * KB // 2, (j // 2 + 1) * KB // 2) if j % 2 else []

        def weights_lo(engine, w, b):
            raw, hi, lo = weight_parts(w, b)
            engine.tensor_tensor(lo, raw, hi, ALU.subtract).then_inc(w_split, 1)

        with nc.Block() as block:

            @block.sync
            def _(sp):
                def load_weights(w, blocks):
                    for b in blocks:
                        n = block0[w] + b
                        if n >= 3:
                            sp.wait_ge(w_split, n - 2)
                        sp.dma_start(w_raw[:, n % 3], t["w_blocks"][n]).then_inc(w_landed[n % 3], 16)

                def load_piece(s, r, k):
                    q = s.piece0 + k
                    if not (isinstance(r, int) and q < 2):
                        sp.wait_ge(x_split, r * 2 + (q - 1))
                    made = made_by.get(id(s.source))
                    if made is not None:
                        unit = (s.piece + k) // 2
                        for ring in range(4):
                            sp.wait_ge(stored[ring], r * (16 * 2) + 16 * (made.group0 + 8 * (unit + 1)) // 4)
                    sp.dma_start(x_raw(q % 2, s.cols), s.source[r * 2 + (s.piece + k)]).then_inc(x_landed[q % 2], 16)

                sp.sem_inc(y_free, 1)
                load_weights(0, range(3, BLOCKS[0]))
                for i, s in enumerate(segments):
                    w = s.weights
                    if first_of[w] is s and w + 1 < len(BLOCKS):
                        load_weights(w + 1, range(0, 3))
                    repeat(sp, 2, s.pieces - 2, lambda r, k: load_piece(s, r, k))
                    if first_of[w] is s and w + 1 == TOP:
                        load_weights(TOP, range(3, M1))
                    if i + 1 < len(segments):
                        for k in range(2):
                            load_piece(segments[i + 1], 0, k)
                    if last_of[w] is s and w + 1 < TOP:
                        load_weights(w + 1, range(3, BLOCKS[w + 1]))
                sp.wait_ge(stored[3], 16 * STORED_GROUPS // 4)
                sp.dma_start(wt2, t["wt2"]).then_inc(top_landed, 16)

                def load_dense(src):
                    for at in DENSE_BLOCKS:
                        sp.dma_start(dense_raw[at:at + DENSE, :], src).then_inc(dense_landed, 16)

                sp.wait_ge(dense_cleared, 1)
                load_dense(t["W_top1"][H:H + DENSE, :])
                sp.wait_ge(dense_split, 1)
                load_dense(t["dense_t"][0])
                for c in range(CHUNKS):
                    if c + 1 < CHUNKS:
                        sp.wait_ge(dense_split, c + 2)
                        load_dense(t["dense_t"][c + 1])
                    sp.wait_ge(y_out, c + 1)
                    sp.dma_start(t["y"][c], top_ring[0:1, 0, :]).then_inc(y_stored, 16)
                    sp.wait_ge(y_stored, 16 * (c + 1))
                    sp.sem_inc(y_free, 1)
                sp.wait_ge(y_stored, 16 * CHUNKS)

            @block.gpsimd
            def _(pool):
                pool.memset(identity[:], 0.0).then_inc(identity_ready, 1)
                pool.wait_ge(identity_ready, 1)
                pool.affine_select(out=identity[:], in_=identity[:], compare_op=ALU.not_equal, fill=1.0,
                                   base=0, pattern=[[-1, P]], channel_multiplier=1).then_inc(identity_ready, 1)
                for b in range(M1):
                    n = block0[TOP] + b
                    pool.wait_ge(w_landed[n % 3], 16 * (n // 3 + 1))
                    pool.tensor_scalar(w_raw[:, n % 3], w_raw[:, n % 3], 1.0 / SUMMANDS, None, ALU.mult).then_inc(w_scaled, 1)
                    pool.wait_ge(w_rounded, n + 1)
                    if b == 0:
                        pool.wait_ge(w_split, block0[TOP])
                    weights_lo(pool, TOP, b)

                pool.wait_ge(consts_landed, 16 * 2)
                pool.wait_ge(w_split, block0[-1])
                pool.wait_ge(biased, BIASED_ALL)

                def lookup(slot, c, tile, fields):
                    pool.sem_inc(slot_taken, 1)
                    for j, f in enumerate(fields):
                        index = ids_now[:, c % 2, tile * FIELDS + f:tile * FIELDS + f + 1]
                        src = t["tables"][f] if f in REMAINING_FIELDS else half[f]
                        pool.indirect_dma_start(
                            out=looked[:, slot, j, :], out_offset=None, in_=src,
                            in_offset=bass.IndirectOffsetOnAxis(ap=index.bitcast(U32), axis=0),
                            bounds_check=src.shape[0] - 1, oob_is_err=False,
                        ).then_inc(looked_up[slot], 16)

                def chunk(c):
                    pool.tensor_copy(ids_now[:, c % 2, :], ids[:, c, :]).then_inc(ids_ready, 1)
                    pool.wait_ge(ids_ready, c + 1)
                    turned_at = lambda source, tile: PER_CHUNK * c + source * TILES * 2 + 2 * (tile + 1)
                    for tile in range(TILES):
                        if c and tile % 2 == 0:
                            pool.wait_ge(turned, turned_at(AND, 2 + tile // 2) - PER_CHUNK)
                        elif c:
                            pool.wait_ge(and_summed, 4 * (c - 1) + 2 + tile // 2 + 1)
                        elif tile == 2:
                            pool.wait_ge(x_split, ALL_PIECES)
                        lookup(tile, c, tile, REMAINING_FIELDS)
                    if c == 0:
                        for ring in range(4):
                            pool.wait_ge(stored[ring], 16 * STORED_GROUPS // 4)
                    for tile in range(TILES):
                        pool.wait_ge(turned, turned_at(REMAINING, tile))
                        lookup(tile, c, tile, ORS)
                    for tile in range(TILES):
                        for second, fields in enumerate((ANDS[0:2], ANDS[2:4])):
                            slot = (2 * tile + second) % 4
                            if tile < 2:
                                pool.wait_ge(turned, turned_at(OR, slot))
                            elif second:
                                pool.wait_ge(and_summed, 4 * c + tile - 2 + 1)
                            else:
                                pool.wait_ge(turned, turned_at(AND, tile - 2))
                            lookup(slot, c, tile, fields)
                for c in range(CHUNKS):
                    chunk(c)

            @block.scalar
            def _(act):
                act.dma_start(columns[:], t["columns"]).then_inc(consts_landed, 16)
                act.dma_start(ids[:], t["ids"]).then_inc(consts_landed, 16)
                act.dma_start(bias_row, t["bo1"].partition_broadcast(P)).then_inc(bias_landed, 16)
                act.sem_inc(bank_free, 4)
                act.sem_inc(h1_out, 4)

                def evacuate(s, i, r, k, j):
                    per = s.groups_per_unit
                    g = s.group0 + k * per + j
                    ring = g % 4
                    act.wait_ge(products, r * (2 * per) + (g + 1))
                    if not (isinstance(r, int) and g < 4):
                        act.wait_ge(stored[ring], r * (16 * 2 * per // 4) + 16 * (g // 4))
                    if s.kind == "columns":
                        func, col = s.func
                        act.activation(out_ring[:, ring, 0:2 * COLS], bank[ring][:, 0:2 * COLS], func,
                                       bias=columns[:, col + j:col + j + 1]).then_inc(bank_free, 1)
                        dst = s.target.rearrange("(u a) p m c -> u m p a c", a=2)[r * 2 + k, j]
                        src = out_ring[:, ring, 0:2 * COLS].rearrange("p (a c) -> p a c", a=2)
                    else:
                        src = out_ring[0:s.tile, ring, :]
                        act.activation(src, bank[ring][0:s.tile, :], ACT.Copy).then_inc(bank_free, 1)
                        side, tile = j // 2, j % 2
                        dst = rows_of(s.target)[r * 4 + (2 * k + tile), :, side * WIDE:(side + 1) * WIDE]
                    if s.bias:
                        act.wait_ge(biased, r * (2 * per) + (BIASED[i] + k * per + j + 1))
                    else:
                        act.wait_ge(bank_free, r * (2 * per) + (4 + g + 1))
                    act.dma_start(dst, src).then_inc(stored[ring], 16)

                def weights_hi(w, b):
                    n = block0[w] + b
                    raw, hi, _ = weight_parts(w, b)
                    if w == TOP:
                        act.wait_ge(w_scaled, b + 1)
                    else:
                        act.wait_ge(w_landed[n % 3], 16 * (n // 3 + 1))
                    act.activation(hi, raw, ACT.Copy).then_inc(w_rounded, 1)

                def next_weights(s, j):
                    w = s.weights + 1
                    for b in blocks_after(s, j) if w < TOP else ():
                        weights_hi(w, b)

                def fold(s, r, k, j):
                    g = s.group0 + k * 2 + j
                    act.wait_ge(products, r * 4 + (g + 1))
                    act.activation(w_hi[:, 2 * k + j, s.target * N1:(s.target + 1) * N1], bank[g % 4][:],
                                   ACT.Copy).then_inc(fold_rounded, 1)
                    act.wait_ge(fold_split, g - segments[8].group0 + 1)
                    act.sem_inc(bank_free, 1)

                for b in range(BLOCKS[0]):
                    weights_hi(0, b)
                act.wait_ge(consts_landed, 32)
                for i, s in enumerate(segments):
                    if s.kind == "fold":
                        for k in range(s.units - (s is segments[-1])):
                            for j in range(2):
                                fold(s, 0, k, j)
                        continue
                    if i == first_and:
                        act.wait_ge(biased, BIASED[i])
                        act.dma_start(bias_row, t["ba1"].partition_broadcast(P)).then_inc(bias_landed, 16)
                    per = s.groups_per_unit
                    unit = lambda r, k: [evacuate(s, i, r, k, j) for j in range(per)]
                    last = s is last_of[s.weights]
                    first = 1 if i == 0 else 0
                    if first:
                        unit(0, 0)
                    if s is first_of[TOP - 1]:
                        for k in range(s.units):
                            unit(0, k)
                            if k < M1:
                                weights_hi(TOP, k)
                        continue
                    repeat(act, first, s.units - last - first, unit)
                    if last:
                        for j in range(per):
                            evacuate(s, i, 0, s.units - 1, j)
                            next_weights(s, j)

                def turn_hi(c, source, tile):
                    func = ACT.Relu if source == OR else ACT.Copy
                    cb = (C_UNIT + SOURCES * c + source) % 2
                    for h in range(2):
                        n = PER_CHUNK * c + (source * TILES + tile) * 2 + h
                        act.wait_ge(turned, n + 1)
                        act.activation(x_hi[:, cb, 4 * h:4 * h + 4, tile * P:(tile + 1) * P],
                                       bank[4 + h][:].rearrange("p (b c) -> p b c", b=4), func).then_inc(turned_hi, 1)

                def relu_second(c, tile):
                    slot = (2 * tile + 1) % 4
                    act.wait_ge(added, 4 * c + tile + 1)
                    act.activation(looked[:, slot, 0, :], looked[:, slot, 0, :], ACT.Relu).then_inc(relued, 1)

                def h1_block(c, m):
                    act.wait_ge(h1_done, M1 * c + m + 1)
                    if c == 0 and m == 0:
                        act.wait_ge(b2_step, 6)
                        for ring in range(4):
                            act.wait_ge(stored[ring], 16 * STORED_GROUPS // 4)
                    if m == 0:
                        act.wait_ge(y_free, c + 1)
                    if m >= 2:
                        act.wait_ge(h1_used, (M1 - 2) * c + m - 1)
                    act.activation(top_ring[:, m % 2, :], bank[m][:], ACT.Relu,
                                   bias=bias1[:, m:m + 1]).then_inc(h1_out, 1)

                def h2_blocks(c):
                    for m in range(M2):
                        act.wait_ge(h2_done, M2 * c + m + 1)
                        act.activation(top_ring[:, m, :], bank[6 + m][:], ACT.Relu,
                                       bias=columns[:, COL_BT2 + m:COL_BT2 + m + 1]).then_inc(h2_out, 1)

                def y_row(c):
                    act.wait_ge(y_done, c + 1)
                    act.activation(top_ring[0:1, 0, :], bank[6][0:1, :], ACT.Copy).then_inc(y_out, 1)

                for name, *at in batch_steps:
                    if name == "fold":
                        fold(segments[-1], 0, segments[-1].units - 1, *at)
                    elif name == "turn":
                        following = next_turn.get(tuple(at))
                        if following and following[1] == AND:
                            relu_second(following[0], following[2])
                        turn_hi(*at)
                    elif name == "multiply" and at[1] == AND:
                        h1_block(at[0], at[2])
                    elif name == "top2" and at[1] == M1 - 1:
                        h2_blocks(at[0])
                    elif name == "top3":
                        y_row(at[0])

            @block.vector
            def _(dve):
                dve.sem_inc(turned_lo, 2)

                def split(s, r, k, pieces=None):
                    u = s.unit0 + k
                    buffer = u % 2
                    if not (isinstance(r, int) and u < 2):
                        per = s.groups_per_unit
                        if k >= 2:
                            dve.wait_ge(products, r * (2 * per) + (s.group0 + (k - 1) * per))
                        else:
                            before = segments[segments.index(s) - 1]
                            dve.wait_ge(products, before.group_end - (1 - k) * before.groups_per_unit)
                    for a in range(s.pieces_per_unit) if pieces is None else pieces:
                        q = s.piece0 + k * s.pieces_per_unit + a
                        step = 2 * s.pieces_per_unit
                        cols = slice(a * s.cols, (a + 1) * s.cols)
                        dve.wait_ge(x_landed[q % 2], r * (16 * step // 2) + 16 * (q // 2 + 1))
                        dve.tensor_copy(x_hi[:, buffer, :, cols], x_raw(q % 2, s.cols)).then_inc(x_rounded, 1)
                        dve.wait_ge(x_rounded, r * step + (q + 1))
                        dve.tensor_tensor(x_lo[:, buffer, :, cols], x_raw(q % 2, s.cols), x_hi[:, buffer, :, cols],
                                          ALU.subtract).then_inc(x_split, 1)

                def add_bias(s, i, r, k, j):
                    g = s.group0 + k * 4 + j
                    side = j // 2
                    dve.wait_ge(bank_free, r * 8 + (4 + g + 1))
                    tile = out_ring[0:s.tile, g % 4, :]
                    dve.tensor_tensor(tile, tile, bias_row[0:s.tile, side * WIDE:(side + 1) * WIDE],
                                      ALU.add).then_inc(biased, 1)

                def fold_lo(s, k, j):
                    g = s.group0 + k * 2 + j
                    cols = slice(s.target * N1, (s.target + 1) * N1)
                    dve.wait_ge(fold_rounded, g - segments[8].group0 + 1)
                    dve.tensor_tensor(w_lo[:, 2 * k + j, cols], bank[g % 4][:], w_hi[:, 2 * k + j, cols],
                                      ALU.subtract).then_inc(fold_split, 1)

                def next_weights_lo(s, j):
                    w = s.weights + 1
                    if w == TOP or s is not last_of[s.weights]:
                        return
                    for b in blocks_after(s, j):
                        dve.wait_ge(w_rounded, block0[w] + b + 1)
                        weights_lo(dve, w, b)

                def split_dense(parts, lo_block, n):
                    dve.wait_ge(dense_landed, 16 * len(DENSE_BLOCKS) * (n + 1))
                    dve.tensor_copy(parts[:], dense_raw).then_inc(dense_rounded, 1)
                    block = slice(DENSE_BLOCKS[lo_block], DENSE_BLOCKS[lo_block] + DENSE)
                    dve.wait_ge(dense_rounded, n + 1)
                    dve.tensor_tensor(parts[block, :], dense_raw[block, :], parts[block, :], ALU.subtract).then_inc(dense_split, 1)

                def split_features(c):
                    if c:
                        dve.wait_ge(dense_used, c)
                    split_dense(dense_x, 1, 1 + c)

                split(segments[0], 0, 0, pieces=[0])
                for b in range(KB):
                    dve.wait_ge(w_rounded, b + 1)
                    weights_lo(dve, 0, b)
                    if b == 0:
                        split(segments[0], 0, 0, pieces=[1])
                split(segments[0], 0, 1)
                dve.wait_ge(consts_landed, 32)
                dve.scalar_tensor_tensor(out=b2[:], in0=columns[:, COL_BA2:COL_BA2 + KB], scalar=float(len(ANDS) // 2),
                                         in1=columns[:, COL_BO2:COL_BO2 + KB], op0=ALU.mult, op1=ALU.add).then_inc(b2_step, 1)
                dve.wait_ge(b2_step, 1)
                dve.tensor_copy(b2_parts[:, :, 0], b2[:]).then_inc(b2_step, 1)
                dve.wait_ge(b2_step, 2)
                dve.tensor_tensor(b2_parts[:, :, 1], b2[:], b2_parts[:, :, 0], ALU.subtract).then_inc(b2_step, 1)

                for i, s in enumerate(segments):
                    if s.bias:
                        dve.wait_ge(bias_landed, 16 if s.bias == "bo1" else 32)

                    def own(k, r=0, last=False):
                        for j in range(s.groups_per_unit):
                            if s.bias:
                                add_bias(s, i, r, k, j)
                            elif s.kind == "fold":
                                fold_lo(s, k, j)
                            if last:
                                next_weights_lo(s, j)

                    def step(r, k):
                        own(k, r)
                        split(s, r, k + 2)
                    if s is segments[-2]:
                        dve.wait_ge(stored[2], 16 * STORED_GROUPS // 4)
                        dve.memset(dense_raw, 0.0).then_inc(dense_cleared, 1)
                    if s.kind == "fold":
                        for k in range(s.units - 2):
                            step(0, k)
                    else:
                        repeat(dve, 0, s.units - 2, step)
                    own(s.units - 2)
                    if i + 1 < len(segments):
                        split(segments[i + 1], 0, 0)
                        own(s.units - 1, last=True)
                        split(segments[i + 1], 0, 1)
                def bias_rows_out():
                    dve.wait_ge(stored[1], 16 * STORED_GROUPS // 4)
                    dve.wait_ge(b2_product, 1)
                    dve.tensor_copy(bias_rows, bank[7][0:2, :]).then_inc(b2_step, 1)

                def first_bias():
                    dve.wait_ge(b2_product, 2)
                    dve.tensor_reduce(bias1[:], bank[7][:, 0:2 * M1].rearrange("p (m two) -> p m two", two=2),
                                      AX.X, ALU.add).then_inc(b2_step, 1)
                    dve.wait_ge(b2_step, 5)
                    dve.tensor_tensor(bias1[:], bias1[:], columns[:, COL_BT1:COL_BT1 + M1], ALU.add).then_inc(b2_step, 1)

                def add_rows(c, source, tile):
                    if source != AND:
                        slots = [tile]
                        use = c * 4 + source
                    else:
                        slots = [(2 * tile + 1) % 4, (2 * tile) % 4]
                        use = c * 4 + 2 + tile // 2
                    for n, slot in enumerate(slots):
                        dve.wait_ge(looked_up[slot], 32 * (use + 1))
                        a, b = looked[:, slot, 0, :], looked[:, slot, 1, :]
                        op = dve.tensor_tensor(a, a, b, ALU.add)
                        if source != AND:
                            op.then_inc(summed, 1)
                        elif n == 0:
                            op.then_inc(added, 1)
                        else:
                            op.then_inc(first_added, 1)
                            dve.wait_ge(first_added, 4 * c + tile + 1)
                            dve.wait_ge(relued, 4 * c + tile + 1)
                            dve.scalar_tensor_tensor(out=a, in0=a, scalar=0.0, in1=looked[:, slots[0], 0, :],
                                                     op0=ALU.max, op1=ALU.add).then_inc(and_summed, 1)

                def turn_lo(c, source, tile):
                    cb = (C_UNIT + SOURCES * c + source) % 2
                    for h in range(2):
                        n = PER_CHUNK * c + (source * TILES + tile) * 2 + h
                        where = (slice(None), cb, slice(4 * h, 4 * h + 4), slice(tile * P, (tile + 1) * P))
                        turned_bank = bank[4 + h][:].rearrange("p (b c) -> p b c", b=4)
                        dve.wait_ge(turned_hi, n + 1)
                        if source == OR:
                            dve.scalar_tensor_tensor(out=x_lo[where], in0=turned_bank, scalar=0.0, in1=x_hi[where],
                                                     op0=ALU.max, op1=ALU.subtract).then_inc(turned_lo, 1)
                        else:
                            dve.tensor_tensor(x_lo[where], turned_bank, x_hi[where], ALU.subtract).then_inc(turned_lo, 1)

                split_dense(dense_w, 2, 0)
                add_rows(0, REMAINING, 0)
                for name, *at in batch_steps:
                    if name == "fold":
                        fold_lo(segments[-1], segments[-1].units - 1, *at)
                    elif name == "features":
                        split_features(*at)
                    elif name == "bias_product":
                        bias_rows_out()
                    elif name == "bias_turn":
                        first_bias()
                    elif name == "turn":
                        following = next_turn.get(tuple(at))
                        if following:
                            add_rows(*following)
                        turn_lo(*at)

            @block.tensor
            def _(pe):

                def three_passes(out, stationary, moving, start, stop):
                    (s_hi, s_lo), (m_hi, m_lo) = stationary, moving
                    pe.matmul(out, s_hi, m_hi, start=start, stop=False)
                    pe.matmul(out, s_hi, m_lo, start=False, stop=False)
                    return pe.matmul(out, s_lo, m_hi, start=False, stop=stop)

                def unit(s, r, k, only=None, first=False):
                    per = s.groups_per_unit
                    buffer = (s.unit0 + k) % 2
                    if not first:
                        pe.wait_ge(x_split, r * (2 * s.pieces_per_unit) + (s.piece0 + (k + 1) * s.pieces_per_unit))
                    for j in range(per) if only is None else [only]:
                        g = s.group0 + k * per + j
                        pe.wait_ge(bank_free, r * (2 * per) + (g + 1))
                        if s.kind == "columns":
                            pe.wait_ge(w_split, block0[s.weights] + j + 1)
                        elif j == 0:
                            pe.wait_ge(w_split, block0[s.weights] + (KB // 2 if s.kind == "rows" else M1))
                        elif j == 2:
                            pe.wait_ge(w_split, block0[s.weights] + KB)
                        if first and j == 0:
                            for a in range(s.pieces_per_unit):
                                pe.wait_ge(x_split, a + 1)
                                rows = slice(a * COLS, (a + 1) * COLS)
                                for kb in range(KB):
                                    last = three_passes(bank[0][:, rows], (w_hi[:, kb, 0:P], w_lo[:, kb, 0:P]),
                                                        (x_hi[:, 0, kb, rows], x_lo[:, 0, kb, rows]), kb == 0, kb == KB - 1)
                        for kb in range(0 if first and j == 0 else KB):
                            if s.kind == "columns":
                                cols = slice(j * P, (j + 1) * P)
                                stationary = w_hi[:, kb, cols], w_lo[:, kb, cols]
                                moving = x_hi[:, buffer, kb, 0:2 * COLS], x_lo[:, buffer, kb, 0:2 * COLS]
                                out = bank[g % 4][:, 0:2 * COLS]
                            else:
                                side, tile = (j // 2, j % 2) if s.kind == "rows" else (0, j)
                                rows = slice(tile * s.tile, (tile + 1) * s.tile)
                                cols = slice(side * WIDE, (side + 1) * WIDE)
                                out = bank[g % 4][0:s.tile, :]
                                stationary = x_hi[:, buffer, kb, rows], x_lo[:, buffer, kb, rows]
                                moving = (w_hi[:, kb, cols], w_lo[:, kb, cols]) if s.kind == "rows" else (z_hi[:, kb, :], z_lo[:, kb, :])
                            last = three_passes(out, stationary, moving, kb == 0, kb == KB - 1)
                        last.then_inc(products, 1)

                for s in segments:
                    at = 0
                    if s is segments[0]:
                        unit(s, 0, 0, first=True)
                        at = 1
                    repeat(pe, at, s.units - at - (s is segments[-1]), lambda r, k: unit(s, r, k))

                def bias_product():
                    pe.wait_ge(b2_step, 3)
                    for kb in range(KB):
                        for part, z in enumerate((z_hi, z_lo)):
                            last = pe.matmul(bank[7][0:2, :], b2_parts[:, kb, :], z[:, kb, :],
                                             start=(kb == 0 and part == 0), stop=(kb == KB - 1 and part == 1))
                    last.then_inc(b2_product, 1)

                def bias_turn():
                    pe.wait_ge(b2_step, 4)
                    for m in range(M1):
                        last = pe.transpose(bank[7][:, 2 * m:2 * m + 2], bias_rows[:, m * P:(m + 1) * P], identity[0:2, 0:2])
                    last.then_inc(b2_product, 1)

                pe.wait_ge(identity_ready, 2)

                def turn(c, source, tile):
                    if source == AND:
                        pe.wait_ge(and_summed, 4 * c + tile + 1)
                        slot = (2 * tile) % 4
                    else:
                        pe.wait_ge(summed, c * 2 * TILES + source * TILES + tile + 1)
                        slot = tile
                    for h in range(2):
                        n = PER_CHUNK * c + (source * TILES + tile) * 2 + h
                        pe.wait_ge(turned_lo, n + 1)
                        for b in range(4):
                            kb = 4 * h + b
                            last = pe.transpose(bank[4 + h][:, b * P:(b + 1) * P],
                                                looked[:, slot, 0, kb * P:(kb + 1) * P], identity[:])
                        last.then_inc(turned, 1)

                def multiply(c, source, m):
                    cb = (C_UNIT + SOURCES * c + source) % 2
                    hi, lo, at = [(z_hi, z_lo, 0), (w_hi, w_lo, N1), (w_hi, w_lo, 0)][source]
                    cols = slice(at + m * P, at + (m + 1) * P)
                    if m == 0:
                        pe.wait_ge(turned_lo, 2 + PER_CHUNK * c + (source + 1) * TILES * 2)
                    if source == REMAINING:
                        pe.wait_ge(h1_out, M1 * c + m + 1)
                        if m == 0:
                            pe.wait_ge(dense_split, 1 + c + 1)
                        if c == 0 and m == 0:
                            pe.wait_ge(bank_free, 4 + GROUPS)
                        op = pe.matmul(bank[m][:], dense_w[0:DENSE_ROWS, m * P:(m + 1) * P], dense_x[0:DENSE_ROWS, :],
                                       start=True, stop=False)
                        if m == M1 - 1:
                            op.then_inc(dense_used, 1)
                    for kb in range(KB):
                        last = three_passes(bank[m][:], (hi[:, kb, cols], lo[:, kb, cols]),
                                            (x_hi[:, cb, kb, :], x_lo[:, cb, kb, :]), False,
                                            source == AND and kb == KB - 1)
                    if source == AND:
                        last.then_inc(h1_done, 1)

                def top2(c, kb):
                    pe.wait_ge(h1_out, 4 + M1 * c + kb + 1)
                    if kb == 0 and c == 0:
                        pe.wait_ge(top_landed, 16)
                        pe.wait_ge(b2_step, 5)
                    elif kb == 0:
                        pe.wait_ge(y_out, c)
                    for m in range(M2):
                        last = pe.matmul(bank[6 + m][:], wt2[:, kb, m * P:(m + 1) * P], top_ring[:, kb % 2, :],
                                         start=(kb == 0), stop=(kb == M1 - 1))
                        if kb == M1 - 1:
                            last.then_inc(h2_done, 1)
                        elif kb < M1 - 2 and m == M2 - 1:
                            last.then_inc(h1_used, 1)

                def top3(c):
                    for m in range(M2):
                        pe.wait_ge(h2_out, M2 * c + m + 1)
                        last = pe.matmul(bank[6][0:1, :], columns[:, COL_WT3 + m:COL_WT3 + m + 1], top_ring[:, m, :],
                                         start=(m == 0), stop=(m == M2 - 1))
                    last.then_inc(y_done, 1)

                def fold(j):
                    unit(segments[-1], 0, segments[-1].units - 1, only=j)

                do = {"features": lambda c: None,
                      "fold": fold, "bias_product": bias_product, "bias_turn": bias_turn, "turn": turn, "multiply": multiply, "top2": top2, "top3": top3}
                for name, *at in batch_steps:
                    do[name](*at)


def general_path(nc, picks_i, picks, first_loads, t):
    def blocked(first):
        w = t["w_blocks"][first * KB:(first + 1) * KB].rearrange("b p k c -> k p b c")
        return [w[kb] for kb in range(KB)]

    def plain(w):
        return [w[r:min(r + P, w.shape[0]), :] for r in range(0, w.shape[0], P)]

    not_layers = [("not1", blocked(0), H), ("not2", blocked(1), H)]
    layers = (not_layers * len(NOTS)
              + [("and", blocked(4) + blocked(5), H)] * (len(ANDS) // 2)
              + [("or", blocked(2) + blocked(3), H)] * (len(ORS) // 2)
              + [("and2", plain(t["Wa2"]), H), ("or2", plain(t["Wo2"]), H),
                 ("top1", plain(t["W_top1"]), N1),
                 ("top2", [t["wt2"][:, kb, :] for kb in range(M1)], N2),
                 ("top3", plain(t["W_top3"]), 1)])
    LAYERS = len(layers)
    WRING = 3
    WBLOCKS = sum(len(w) for _, w, _ in layers)
    assert WBLOCKS % WRING == 0
    blocks_until = [sum(len(w) for _, w, _ in layers[:n + 1]) for n in range(LAYERS)]
    COPIES = LAYERS + 1
    NTILES = BATCH // P
    DVE_STEPS = 42

    with ExitStack() as ctx:
        sb = lambda name, shape, dt=F32: ctx.enter_context(nc.sbuf_tensor(name, shape, dt))
        sem = lambda name: ctx.enter_context(nc.semaphore(name))
        iv = sb("iv", [P, FIELDS, H])
        g_ids = sb("g_ids", [P, NTILES, FIELDS], I32)
        g_ids_now = sb("g_ids_now", [P, FIELDS], I32)
        rows = sb("rows", [P, 2, H])
        rows_t = sb("rows_t", [P, 2 * KB, P])
        weights = sb("weights", [P, WRING, H])
        sum_t = sb("sum_t", [P, H])
        tanh_rows = sb("tanh_rows", [P, 2, H])
        u_sum = sb("u_sum", [P, 2, H])
        bias = {name: sb("row_" + name, [P, t[name].shape[0]]) for name in ("bn1", "bn2", "ba1", "bo1", "ba2", "bo2", "b_top1", "b_top2")}
        dense_sb = sb("dense_sb", [P, DENSE])
        g_identity = sb("g_identity", [P, P])
        y_rows = sb("y_rows", [P, 1])
        paired = len(ANDS) + len(ORS)
        field_no = sb("field_no", [P, FIELDS])
        hits = sb("hits", [P, paired, FIELDS])
        processed = sb("processed", [P, FIELDS])
        remaining = sb("remaining", [P, FIELDS])
        count = sb("count", [P, 1])
        count_all = sb("count_all", [P, 1])
        inv_count = sb("inv_count", [P, 1])
        turned_ps = ctx.enter_context(nc.psum_tensor("turned_ps", [P, 2 * KB * P], F32))
        out_ps = ctx.enter_context(nc.psum_tensor("out_ps", [P, H], F32))

        g_consts = sem("g_consts")
        g_identity_ready = sem("g_identity_ready")
        g_ids_ready = sem("g_ids_ready")
        lookups_begun = sem("lookups_begun")
        gathered = sem("gathered")
        dense_rows = sem("dense_rows")
        g_w_landed = [sem(f"g_w_landed{i}") for i in range(WRING)]
        w_used = sem("w_used")
        ready = sem("ready")
        g_turned = sem("g_turned")
        copied = sem("copied")
        tanh_input, tanh_done = sem("tanh_input"), sem("tanh_done")
        y_ready, g_y_stored = sem("y_ready"), sem("g_y_stored")
        tile_done = sem("tile_done")
        dve_step = sem("dve_step")
        counting = sem("counting")
        picking = sem("picking")
        y_tiles = t["y_rows"].rearrange("(n p) o -> n p o", p=P)
        dense_tiles = t["dense_ctx"].rearrange("(n p) d -> n p d", p=P)

        with nc.Block() as block:

            @block.sync
            def _(sp):
                first_loads.wait(sp)
                for name, tile in bias.items():
                    sp.dma_start(tile[:], t[name].partition_broadcast(P)).then_inc(g_consts, 16)
                sp.dma_start(g_ids[:], t["ids"].rearrange("p c (n f) -> p (c n) f", f=FIELDS)).then_inc(g_consts, 16)
                with sp.Fori(0, NTILES) as i:
                    sp.wait_ge(tile_done, i + 1)
                    sp.dma_start(dense_sb[:], dense_tiles[i]).then_inc(dense_rows, 16)
                    n = 0
                    for _, blocks, width in layers:
                        for w in blocks:
                            dst = weights[0:w.shape[0], n % WRING, 0:width]
                            if len(w.shape) == 3:
                                dst = dst.rearrange("p (b c) -> p b c", b=KB)
                            sp.wait_ge(w_used, i * WBLOCKS + (n + 1))
                            sp.dma_start(dst, w).then_inc(g_w_landed[n % WRING], 16)
                            n += 1
                sp.wait_ge(g_y_stored, 16 * NTILES)

            @block.gpsimd
            def _(pool):
                pool.memset(g_identity[:], 0.0).then_inc(g_identity_ready, 1)
                pool.wait_ge(g_identity_ready, 1)
                pool.affine_select(out=g_identity[:], in_=g_identity[:], compare_op=ALU.not_equal, fill=1.0,
                                   base=0, pattern=[[-1, P]], channel_multiplier=1).then_inc(g_identity_ready, 1)
                pool.wait_ge(g_consts, 16 * (len(bias) + 1))
                with pool.Fori(0, NTILES) as i:
                    pool.wait_ge(tile_done, i + 1)
                    pool.tensor_copy(g_ids_now[:], g_ids[:, i, :]).then_inc(g_ids_ready, 1)
                    pool.wait_ge(g_ids_ready, i + 1)
                    pool.sem_inc(lookups_begun, 1)
                    for f in range(FIELDS):
                        pool.indirect_dma_start(
                            out=iv[:, f, :], out_offset=None, in_=t["tables"][f],
                            in_offset=bass.IndirectOffsetOnAxis(ap=g_ids_now[:, f:f + 1].bitcast(U32), axis=0),
                            bounds_check=VOCAB[f] - 1, oob_is_err=False).then_inc(gathered, 16)

            @block.scalar
            def _(act):
                with act.Fori(0, NTILES) as i:
                    copies = tanhs = 0
                    for n, (name, blocks, _) in enumerate(layers):
                        act.wait_ge(g_turned, i * LAYERS + (n + 1))
                        whole = len(blocks) - (name == "top1")
                        act.activation(rows_t[:, 0:whole, :], turned_ps[:, 0:whole * P].rearrange("p (k c) -> p k c", c=P),
                                       ACT.Copy).then_inc(copied, 1)
                        if name == "top1":
                            act.activation(rows_t[0:DENSE, KB, :], turned_ps[0:DENSE, KB * P:(KB + 1) * P],
                                           ACT.Copy).then_inc(copied, 1)
                        if name == "not2":
                            act.wait_ge(tanh_input, i * len(NOTS) + (tanhs + 1))
                            act.activation(tanh_rows[:, tanhs, :], sum_t[:], ACT.Tanh).then_inc(tanh_done, 1)
                            tanhs += 1
                    act.wait_ge(y_ready, i + 1)
                    act.dma_start(y_tiles[i], y_rows[:]).then_inc(g_y_stored, 16)

            @block.tensor
            def _(pe):
                pe.sem_inc(w_used, WRING)
                pe.wait_ge(g_identity_ready, 2)
                with pe.Fori(0, NTILES) as i:
                    copies = used = 0
                    flat = rows[:].rearrange("p a n -> p (a n)")
                    for n, (name, blocks, width) in enumerate(layers):
                        pe.wait_ge(ready, i * LAYERS + (n + 1))
                        for kb, w in enumerate(blocks):
                            size = w.shape[0]
                            last = pe.transpose(turned_ps[0:size, kb * P:(kb + 1) * P], flat[:, kb * P:kb * P + size],
                                                g_identity[:])
                        last.then_inc(g_turned, 1)
                        copies += 1 + (name == "top1")
                        pe.wait_ge(copied, i * COPIES + copies)
                        for kb, w in enumerate(blocks):
                            size, slot = w.shape[0], used % WRING
                            pe.wait_ge(g_w_landed[slot], i * (16 * WBLOCKS // WRING) + 16 * (used // WRING + 1))
                            for at in range(0, width, WIDE):
                                cols = slice(at, min(at + WIDE, width))
                                last = pe.matmul(out_ps[:, cols], rows_t[0:size, kb, :], weights[0:size, slot, cols],
                                                 start=(kb == 0), stop=(kb == len(blocks) - 1))
                            last.then_inc(w_used, 1)
                            used += 1

            @block.vector
            def _(dve):
                for f in range(FIELDS):
                    dve.memset(field_no[:, f:f + 1], float(f)).then_inc(counting, 1)
                dve.wait_ge(counting, FIELDS)
                for e in range(paired):
                    dve.tensor_scalar(hits[:, e, :], field_no[:], picks[:, len(NOTS) + e:len(NOTS) + e + 1], None,
                                      ALU.is_equal).then_inc(counting, 1)
                dve.wait_ge(counting, FIELDS + paired)
                dve.tensor_reduce(processed[:], hits[:].rearrange("p e f -> p f e"), AX.X, ALU.max).then_inc(counting, 1)
                dve.wait_ge(counting, FIELDS + paired + 1)
                dve.tensor_scalar(remaining[:], processed[:], -1.0, 1.0, ALU.mult, ALU.add).then_inc(counting, 1)
                dve.wait_ge(counting, FIELDS + paired + 2)
                dve.tensor_reduce(count[:], remaining[:], AX.X, ALU.add).then_inc(counting, 1)
                dve.wait_ge(counting, FIELDS + paired + 3)
                dve.tensor_scalar(count_all[:], count[:], float(PAIRS), None, ALU.add).then_inc(counting, 1)
                dve.wait_ge(counting, FIELDS + paired + 4)
                dve.reciprocal(inv_count[:], count_all[:]).then_inc(counting, 1)
                dve.wait_ge(counting, FIELDS + paired + 5)
                field = [dve.value_load(picks_i[0:1, e:e + 1], min_val=0, max_val=FIELDS - 1) for e in range(len(STRUCTURE))]
                dve.sem_inc(tile_done, 1)
                dve.wait_ge(g_consts, 16 * (len(bias) + 1))
                with dve.Fori(0, NTILES) as i:
                    steps = [0]

                    def did(op):
                        steps[0] += 1
                        op.then_inc(dve_step, 1)
                        dve.wait_ge(dve_step, i * DVE_STEPS + steps[0])

                    def of_field(e):
                        return iv[:, bass.ds(field[e], 1), :].rearrange("p a n -> p (a n)")

                    def add_bias(name, width=H):
                        did(dve.tensor_tensor(sum_t[:, 0:width], out_ps[:, 0:width], bias[name][:], ALU.add))

                    def rectify(to, width=H):
                        did(dve.tensor_scalar(to, sum_t[:, 0:width], 0.0, None, ALU.max))

                    dve.wait_ge(gathered, i * (16 * FIELDS) + 16 * FIELDS)
                    nots = pairs = 0
                    for n, (name, blocks, _) in enumerate(layers):
                        if name in ("not1", "and", "or"):
                            dve.sem_inc(picking, 1)
                        if name == "not1":
                            did(dve.tensor_copy(rows[:, 0, :], of_field(nots)))
                        elif name in ("and", "or"):
                            if pairs == 0:
                                for s in range(len(NOTS)):
                                    did(dve.tensor_copy(of_field(s), tanh_rows[:, s, :]))
                                    dve.sem_inc(picking, 1)
                            for side in range(2):
                                did(dve.tensor_copy(rows[:, side, :], of_field(len(NOTS) + 2 * pairs + side)))
                                dve.sem_inc(picking, 1)
                        elif name == "and2":
                            did(dve.tensor_copy(rows[:, 0, :], u_sum[:, 0, :]))
                        elif name == "or2":
                            did(dve.tensor_copy(rows[:, 0, :], u_sum[:, 1, :]))
                        elif name == "top1":
                            dve.wait_ge(dense_rows, i * 16 + 16)
                            did(dve.tensor_copy(rows[:, 1, 0:DENSE], dense_sb[:]))
                        dve.sem_inc(ready, 1)
                        dve.wait_ge(w_used, i * WBLOCKS + (WRING + blocks_until[n]))
                        if name == "not1":
                            add_bias("bn1")
                            rectify(rows[:, 0, :])
                        elif name == "not2":
                            add_bias("bn2")
                            dve.sem_inc(tanh_input, 1)
                            dve.wait_ge(tanh_done, i * len(NOTS) + (nots + 1))
                            nots += 1
                        elif name in ("and", "or"):
                            add_bias("ba1" if name == "and" else "bo1")
                            total = u_sum[:, 0 if name == "and" else 1, :]
                            if pairs in (0, len(ANDS) // 2):
                                rectify(total)
                            else:
                                did(dve.scalar_tensor_tensor(out=total, in0=sum_t[:], scalar=0.0, in1=total,
                                                             op0=ALU.max, op1=ALU.add))
                            pairs += 1
                        elif name == "and2":
                            did(dve.scalar_tensor_tensor(out=u_sum[:, 0, :], in0=bias["ba2"][:], scalar=float(len(ANDS) // 2),
                                                         in1=out_ps[:], op0=ALU.mult, op1=ALU.add))
                        elif name == "or2":
                            did(dve.scalar_tensor_tensor(out=sum_t[:], in0=bias["bo2"][:], scalar=float(len(ORS) // 2),
                                                         in1=out_ps[:], op0=ALU.mult, op1=ALU.add))
                            did(dve.tensor_tensor(sum_t[:], sum_t[:], u_sum[:, 0, :], ALU.add))
                            for f in range(FIELDS):
                                did(dve.scalar_tensor_tensor(out=sum_t[:], in0=iv[:, f, :], scalar=remaining[:, f:f + 1],
                                                             in1=sum_t[:], op0=ALU.mult, op1=ALU.add))
                            did(dve.tensor_scalar(rows[:, 0, :], sum_t[:], inv_count[:, 0:1], None, ALU.mult))
                        elif name == "top1":
                            add_bias("b_top1", N1)
                            rectify(rows[:, 0, 0:N1], N1)
                        elif name == "top2":
                            add_bias("b_top2", N2)
                            rectify(rows[:, 0, 0:N2], N2)
                        else:
                            did(dve.tensor_copy(y_rows[:], out_ps[:, 0:1]))
                            dve.sem_inc(y_ready, 1)
                            dve.wait_ge(g_y_stored, i * 16 + 16)
                    dve.sem_inc(tile_done, 1)
                    assert steps[0] == DVE_STEPS, steps[0]


def build(nc, t):
    with ExitStack() as ctx:
        first_loads = FirstLoads(nc, ctx, t)
        picks_i, picks, flag = read_structure(nc, ctx, t["not_idx"], t["and_pairs"], t["or_pairs"], first_loads)
        other = nc.values_load(flag[0:1, 0:1], min_val=0, max_val=1,
                               skip_runtime_bounds_check_because="a comparison's result is 0 or 1")
        with nc.If(other == 0):
            table_path(nc, first_loads, t)
        with nc.Else():
            general_path(nc, picks_i, picks, first_loads, t)


def _pieces(np, table, cols):
    return table.reshape(-1, cols, KB, P).transpose(0, 3, 2, 1)


def _blocks(np, w):
    return w.reshape(KB, P, w.shape[1] // P, P).transpose(2, 1, 0, 3)


def _columns(v):
    return v.reshape(-1, P).T


def kernel(**inputs):
    import numpy as np
    import concourse.bacc as _bacc
    from concourse import mybir as _mybir
    from concourse.bass_utils import run_bass_kernel_spmd as _run

    a = {k: np.asarray(v) for k, v in inputs.items()}
    L = {k[len("L0_rec_"):]: v for k, v in a.items() if k.startswith("L0_rec_")}
    wa, wo = L["Wa1"], L["Wo1"]
    arrays = {
        "x_pieces": np.concatenate([_pieces(np, a[f"tbl_{f}"], COLS) for f in FIELD_ORDER]),
        "fold_pieces": np.concatenate([_pieces(np, L["Wa2"], FOLD_COLS), _pieces(np, L["Wo2"], FOLD_COLS)]),
        "w_blocks": np.concatenate([_blocks(np, w) for w in (L["Wn1"], L["Wn2"], wo[:H], wo[H:], wa[:H], wa[H:],
                                                            a["W_top1"][:H])]),
        "columns": np.concatenate([_columns(v) for v in (L["bn1"], L["bn2"], L["ba2"], L["bo2"], a["b_top1"],
                                                         a["b_top2"], a["W_top3"][:, 0])], axis=1),
        "wt2": a["W_top2"].reshape(M1, P, N2).transpose(1, 0, 2),
        "dense_t": a["dense_ctx"].reshape(CHUNKS, CHUNK, DENSE).transpose(0, 2, 1),
        "ids": a["ids"].reshape(CHUNKS, TILES, P, FIELDS).transpose(2, 0, 1, 3).reshape(P, CHUNKS, TILES * FIELDS),
        "W_top1": a["W_top1"], "bo1": L["bo1"], "ba1": L["ba1"],
        "not_idx": L["not_idx"], "and_pairs": L["and_pairs"], "or_pairs": L["or_pairs"],
    }
    for name in ("bn1", "bn2", "ba2", "bo2", "Wa2", "Wo2"):
        arrays[name] = L[name]
    for name in ["b_top1", "b_top2", "W_top3", "dense_ctx"] + [f"tbl_{f}" for f in range(FIELDS)]:
        arrays[name] = a[name]
    arrays = {k: np.ascontiguousarray(v) for k, v in arrays.items()}
    nc = _bacc.Bacc("TRN2", target_bir_lowering=False, num_devices=1)
    t = {k: nc.dram_tensor(k + "_in", v.shape, _mybir.dt.from_np(v.dtype), kind="ExternalInput").ap()
         for k, v in arrays.items()}
    t["tables"] = [t[f"tbl_{f}"] for f in range(FIELDS)]
    y = nc.dram_tensor("y_out", (BATCH, 1), F32, kind="ExternalOutput").ap()
    t["y_rows"] = y
    t["y"] = y.rearrange("(c n) o -> c o n", n=CHUNK)
    build(nc, t)
    r = _run(nc, [{k + "_in": v for k, v in arrays.items()}], core_ids=[0])
    return r.results[0]["y_out"]
```
